# Optimizing a Trainium2 kernel written in Bass

```python
import numpy as np
import jax
import jax.numpy as jnp

def _softmax(x, axis=-1):
    return jax.nn.softmax(x, axis=axis)

def _gelu(x):
    return jax.nn.gelu(x, approximate=True)

def _silu(x):
    return jax.nn.silu(x)

def _sigmoid(x):
    return jax.nn.sigmoid(x)

def _layernorm(x, axis=-1, eps=1e-05):
    m = jnp.mean(x, axis=axis, keepdims=True)
    v = jnp.var(x, axis=axis, keepdims=True)
    return (x - m) / jnp.sqrt(v + eps)

def _scatter_add(tgt, idx, src, axis=0):
    return tgt.at[idx].add(src)

def _segment_sum(src, seg, n):
    return jax.ops.segment_sum(src, seg, n)
kernel_name = 'mk_dlrm_tower_d1_rec_r8_3b42af'

def setup_inputs(seed: int=0):
    np.random.seed(seed)
    _w = jnp.asarray

    def _rec_inputs():
        import jax
        import jax.numpy as jnp
        _tk = jax.random.key(seed)
        dense_ctx = jax.random.normal(jax.random.fold_in(_tk, 190), (512, 16), jnp.float32)
        ids = jnp.stack([jax.random.randint(jax.random.fold_in(_tk, 200 + f), (512,), 0, v, jnp.int32) for f, v in enumerate([1000, 1250, 1000, 1250, 12500, 12500, 1000, 125000, 1250, 125000, 125000, 12500, 1000, 12500, 1250, 12500, 12500, 1250, 1250, 1250, 1000, 1000, 12500, 1250, 1250, 1000, 1250, 1250, 1250, 1250, 1000, 1000])], axis=1)
        tbl_0 = 0.05 * jax.random.normal(jax.random.fold_in(_tk, 500 + 0), (1000, 64), jnp.float32)
        tbl_1 = 0.05 * jax.random.normal(jax.random.fold_in(_tk, 500 + 1), (1250, 64), jnp.float32)
        tbl_2 = 0.05 * jax.random.normal(jax.random.fold_in(_tk, 500 + 2), (1000, 64), jnp.float32)
        tbl_3 = 0.05 * jax.random.normal(jax.random.fold_in(_tk, 500 + 3), (1250, 64), jnp.float32)
        tbl_4 = 0.05 * jax.random.normal(jax.random.fold_in(_tk, 500 + 4), (12500, 64), jnp.float32)
        tbl_5 = 0.05 * jax.random.normal(jax.random.fold_in(_tk, 500 + 5), (12500, 64), jnp.float32)
        tbl_6 = 0.05 * jax.random.normal(jax.random.fold_in(_tk, 500 + 6), (1000, 64), jnp.float32)
        tbl_7 = 0.05 * jax.random.normal(jax.random.fold_in(_tk, 500 + 7), (125000, 64), jnp.float32)
        tbl_8 = 0.05 * jax.random.normal(jax.random.fold_in(_tk, 500 + 8), (1250, 64), jnp.float32)
        tbl_9 = 0.05 * jax.random.normal(jax.random.fold_in(_tk, 500 + 9), (125000, 64), jnp.float32)
        tbl_10 = 0.05 * jax.random.normal(jax.random.fold_in(_tk, 500 + 10), (125000, 64), jnp.float32)
        tbl_11 = 0.05 * jax.random.normal(jax.random.fold_in(_tk, 500 + 11), (12500, 64), jnp.float32)
        tbl_12 = 0.05 * jax.random.normal(jax.random.fold_in(_tk, 500 + 12), (1000, 64), jnp.float32)
        tbl_13 = 0.05 * jax.random.normal(jax.random.fold_in(_tk, 500 + 13), (12500, 64), jnp.float32)
        tbl_14 = 0.05 * jax.random.normal(jax.random.fold_in(_tk, 500 + 14), (1250, 64), jnp.float32)
        tbl_15 = 0.05 * jax.random.normal(jax.random.fold_in(_tk, 500 + 15), (12500, 64), jnp.float32)
        tbl_16 = 0.05 * jax.random.normal(jax.random.fold_in(_tk, 500 + 16), (12500, 64), jnp.float32)
        tbl_17 = 0.05 * jax.random.normal(jax.random.fold_in(_tk, 500 + 17), (1250, 64), jnp.float32)
        tbl_18 = 0.05 * jax.random.normal(jax.random.fold_in(_tk, 500 + 18), (1250, 64), jnp.float32)
        tbl_19 = 0.05 * jax.random.normal(jax.random.fold_in(_tk, 500 + 19), (1250, 64), jnp.float32)
        tbl_20 = 0.05 * jax.random.normal(jax.random.fold_in(_tk, 500 + 20), (1000, 64), jnp.float32)
        tbl_21 = 0.05 * jax.random.normal(jax.random.fold_in(_tk, 500 + 21), (1000, 64), jnp.float32)
        tbl_22 = 0.05 * jax.random.normal(jax.random.fold_in(_tk, 500 + 22), (12500, 64), jnp.float32)
        tbl_23 = 0.05 * jax.random.normal(jax.random.fold_in(_tk, 500 + 23), (1250, 64), jnp.float32)
        tbl_24 = 0.05 * jax.random.normal(jax.random.fold_in(_tk, 500 + 24), (1250, 64), jnp.float32)
        tbl_25 = 0.05 * jax.random.normal(jax.random.fold_in(_tk, 500 + 25), (1000, 64), jnp.float32)
        tbl_26 = 0.05 * jax.random.normal(jax.random.fold_in(_tk, 500 + 26), (1250, 64), jnp.float32)
        tbl_27 = 0.05 * jax.random.normal(jax.random.fold_in(_tk, 500 + 27), (1250, 64), jnp.float32)
        tbl_28 = 0.05 * jax.random.normal(jax.random.fold_in(_tk, 500 + 28), (1250, 64), jnp.float32)
        tbl_29 = 0.05 * jax.random.normal(jax.random.fold_in(_tk, 500 + 29), (1250, 64), jnp.float32)
        tbl_30 = 0.05 * jax.random.normal(jax.random.fold_in(_tk, 500 + 30), (1000, 64), jnp.float32)
        tbl_31 = 0.05 * jax.random.normal(jax.random.fold_in(_tk, 500 + 31), (1000, 64), jnp.float32)
        _rk = jax.random.fold_in(_tk, 7)
        W_top1 = 0.0693375 * jax.random.normal(jax.random.fold_in(_tk, 801), (208, 512), jnp.float32)
        W_top2 = 0.0441942 * jax.random.normal(jax.random.fold_in(_tk, 802), (512, 256), jnp.float32)
        W_top3 = 0.0625 * jax.random.normal(jax.random.fold_in(_tk, 803), (256, 1), jnp.float32)
        b_top1 = jnp.zeros((512,), jnp.float32)
        b_top2 = jnp.zeros((256,), jnp.float32)
        return (dense_ctx, ids, tbl_0, tbl_1, tbl_2, tbl_3, tbl_4, tbl_5, tbl_6, tbl_7, tbl_8, tbl_9, tbl_10, tbl_11, tbl_12, tbl_13, tbl_14, tbl_15, tbl_16, tbl_17, tbl_18, tbl_19, tbl_20, tbl_21, tbl_22, tbl_23, tbl_24, tbl_25, tbl_26, tbl_27, tbl_28, tbl_29, tbl_30, tbl_31, W_top1, b_top1, W_top2, b_top2, W_top3)
    dense_ctx, ids, tbl_0, tbl_1, tbl_2, tbl_3, tbl_4, tbl_5, tbl_6, tbl_7, tbl_8, tbl_9, tbl_10, tbl_11, tbl_12, tbl_13, tbl_14, tbl_15, tbl_16, tbl_17, tbl_18, tbl_19, tbl_20, tbl_21, tbl_22, tbl_23, tbl_24, tbl_25, tbl_26, tbl_27, tbl_28, tbl_29, tbl_30, tbl_31, W_top1, b_top1, W_top2, b_top2, W_top3 = _rec_inputs()

    def _L0_rec_setup():
        import jax, jax.numpy as jnp
        import numpy as np
        F0 = 32
        D = 64
        B = 256

        def _cin_layer(h, h0, W, b):
            Hn = h.shape[1]
            Mn = h0.shape[1]
            Wr = W.reshape(W.shape[0], Hn, Mn)
            x = jnp.einsum('bhd,bmd,ohm->bod', h, h0, Wr) + b[None, :, None]
            return jax.nn.relu(x)
        key = jax.random.key(seed)
        k1, k2, k3 = jax.random.split(key, 3)
        inputs = jax.random.normal(k1, (B, F0, D), dtype=jnp.float32)
        W1 = jax.random.normal(k2, (128, F0 * F0), dtype=jnp.float32) * (1.0 / np.sqrt(F0 * F0))
        b1 = jnp.zeros((128,), dtype=jnp.float32)
        W2 = jax.random.normal(k3, (128, 64 * F0), dtype=jnp.float32) * (1.0 / np.sqrt(64 * F0))
        b2 = jnp.zeros((128,), dtype=jnp.float32)
        return {'inputs': inputs, 'W1': W1, 'b1': b1, 'W2': W2, 'b2': b2}
    _L0_rec_all = _L0_rec_setup()
    _L0_rec_in = {k: v for k, v in _L0_rec_all.items() if k in ('W1', 'b1', 'W2', 'b2')}
    del _L0_rec_all
    return {'dense_ctx': dense_ctx, 'ids': ids, 'tbl_0': tbl_0, 'tbl_1': tbl_1, 'tbl_2': tbl_2, 'tbl_3': tbl_3, 'tbl_4': tbl_4, 'tbl_5': tbl_5, 'tbl_6': tbl_6, 'tbl_7': tbl_7, 'tbl_8': tbl_8, 'tbl_9': tbl_9, 'tbl_10': tbl_10, 'tbl_11': tbl_11, 'tbl_12': tbl_12, 'tbl_13': tbl_13, 'tbl_14': tbl_14, 'tbl_15': tbl_15, 'tbl_16': tbl_16, 'tbl_17': tbl_17, 'tbl_18': tbl_18, 'tbl_19': tbl_19, 'tbl_20': tbl_20, 'tbl_21': tbl_21, 'tbl_22': tbl_22, 'tbl_23': tbl_23, 'tbl_24': tbl_24, 'tbl_25': tbl_25, 'tbl_26': tbl_26, 'tbl_27': tbl_27, 'tbl_28': tbl_28, 'tbl_29': tbl_29, 'tbl_30': tbl_30, 'tbl_31': tbl_31, 'W_top1': W_top1, 'b_top1': b_top1, 'W_top2': W_top2, 'b_top2': b_top2, 'W_top3': W_top3, 'L0_rec_W1': _L0_rec_in['W1'], 'L0_rec_b1': _L0_rec_in['b1'], 'L0_rec_W2': _L0_rec_in['W2'], 'L0_rec_b2': _L0_rec_in['b2']}

def reference(dense_ctx, ids, tbl_0, tbl_1, tbl_2, tbl_3, tbl_4, tbl_5, tbl_6, tbl_7, tbl_8, tbl_9, tbl_10, tbl_11, tbl_12, tbl_13, tbl_14, tbl_15, tbl_16, tbl_17, tbl_18, tbl_19, tbl_20, tbl_21, tbl_22, tbl_23, tbl_24, tbl_25, tbl_26, tbl_27, tbl_28, tbl_29, tbl_30, tbl_31, W_top1, b_top1, W_top2, b_top2, W_top3, L0_rec_W1, L0_rec_b1, L0_rec_W2, L0_rec_b2):
    import jax
    import jax.numpy as jnp

    def _L0_rec_ref(inputs, W1, b1, W2, b2):
        import jax, jax.numpy as jnp
        import numpy as np
        F0 = 32
        D = 64
        B = 256

        def _cin_layer(h, h0, W, b):
            Hn = h.shape[1]
            Mn = h0.shape[1]
            Wr = W.reshape(W.shape[0], Hn, Mn)
            x = jnp.einsum('bhd,bmd,ohm->bod', h, h0, Wr) + b[None, :, None]
            return jax.nn.relu(x)
        h0 = inputs
        x1 = _cin_layer(h0, h0, W1, b1)
        next_hidden = x1[:, :64]
        direct1 = x1[:, 64:]
        direct2 = _cin_layer(next_hidden, h0, W2, b2)
        result = jnp.concatenate([direct1, direct2], axis=1)
        return jnp.sum(result, axis=-1)
    e = jnp.stack([tbl_0[ids[:, 0]], tbl_1[ids[:, 1]], tbl_2[ids[:, 2]], tbl_3[ids[:, 3]], tbl_4[ids[:, 4]], tbl_5[ids[:, 5]], tbl_6[ids[:, 6]], tbl_7[ids[:, 7]], tbl_8[ids[:, 8]], tbl_9[ids[:, 9]], tbl_10[ids[:, 10]], tbl_11[ids[:, 11]], tbl_12[ids[:, 12]], tbl_13[ids[:, 13]], tbl_14[ids[:, 14]], tbl_15[ids[:, 15]], tbl_16[ids[:, 16]], tbl_17[ids[:, 17]], tbl_18[ids[:, 18]], tbl_19[ids[:, 19]], tbl_20[ids[:, 20]], tbl_21[ids[:, 21]], tbl_22[ids[:, 22]], tbl_23[ids[:, 23]], tbl_24[ids[:, 24]], tbl_25[ids[:, 25]], tbl_26[ids[:, 26]], tbl_27[ids[:, 27]], tbl_28[ids[:, 28]], tbl_29[ids[:, 29]], tbl_30[ids[:, 30]], tbl_31[ids[:, 31]]], axis=1)
    z = _L0_rec_ref(e, L0_rec_W1, L0_rec_b1, L0_rec_W2, L0_rec_b2)
    z = z.reshape(z.shape[0], -1)
    h = jnp.concatenate([z, dense_ctx], axis=1)
    h = jnp.maximum(h @ W_top1 + b_top1, 0.0)
    h = jnp.maximum(h @ W_top2 + b_top2, 0.0)
    y = h @ W_top3
    return y

_drawn_inputs = setup_inputs


def setup_inputs(seed=0):
    import zlib

    import numpy as np

    out = dict(_drawn_inputs(seed))
    spreads = {'b_top1': (0.0, 2.0),
     'b_top2': (0.0, 2.0),
     'L0_rec_b1': (0.0, 0.322),
     'L0_rec_b2': (0.0, 0.686)}
    factors = {'tbl_0': 8.0,
     'tbl_1': 8.0,
     'tbl_2': 8.0,
     'tbl_3': 8.0,
     'tbl_4': 8.0,
     'tbl_5': 8.0,
     'tbl_6': 8.0,
     'tbl_7': 8.0,
     'tbl_8': 8.0,
     'tbl_9': 8.0,
     'tbl_10': 8.0,
     'tbl_11': 8.0,
     'tbl_12': 8.0,
     'tbl_13': 8.0,
     'tbl_14': 8.0,
     'tbl_15': 8.0,
     'tbl_16': 8.0,
     'tbl_17': 8.0,
     'tbl_18': 8.0,
     'tbl_19': 8.0,
     'tbl_20': 8.0,
     'tbl_21': 8.0,
     'tbl_22': 8.0,
     'tbl_23': 8.0,
     'tbl_24': 8.0,
     'tbl_25': 8.0,
     'tbl_26': 8.0,
     'tbl_27': 8.0,
     'tbl_28': 8.0,
     'tbl_29': 8.0,
     'tbl_30': 8.0,
     'tbl_31': 8.0,
     'L0_rec_W1': 8.0,
     'L0_rec_W2': 8.0,
     'dense_ctx': 8.0}
    for name, (base, spread) in spreads.items():
        noise = np.random.default_rng([zlib.crc32(name.encode()), seed]).standard_normal(out[name].shape)
        drawn = base * np.exp(spread * noise) if base else spread * noise
        out[name] = jnp.asarray(drawn.astype(out[name].dtype))
    for name, factor in factors.items():
        out[name] = (out[name] * factor).astype(out[name].dtype)
    return out
```

```python
import concourse.bass as bass
from concourse import mybir
from contextlib import ExitStack

BATCH, FIELDS, DIM = 512, 32, 64
HIDDEN, DIRECT1, OUT2 = 64, 64, 128
DENSE, TOP1, TOP2 = 16, 512, 256

P = 128
QUAD = 32
BANK = 512
SAMPLES = 16
COLS = SAMPLES * DIM
TILES = BATCH // SAMPLES
PER_GATHER = P // FIELDS
GATHERS = SAMPLES // PER_GATHER
ROTS = FIELDS * HIDDEN // P // 2
CHUNKS1 = 4
CHUNKS2 = 2 * ROTS
SCRATCH_ROWS = 2 * FIELDS

SPLIT2 = (1, 4, 6, 9, 11, 14)
LAG = 2
PLAIN_PER_TILE = CHUNKS1 + CHUNKS2 - len(SPLIT2)
PLAIN_SLOTS = 7
PRODUCT_SLOTS = 3
PART_SLOTS = 4
assert (2 * PLAIN_PER_TILE) % PLAIN_SLOTS == 0
assert (2 * len(SPLIT2)) % PART_SLOTS == 0 and (2 * len(SPLIT2)) % PRODUCT_SLOTS == 0
assert CHUNKS2 - 1 not in SPLIT2


def cin_tower(nc, tables, ids, bases, w1a, w1b, w1c, b1, w2, b2, dense_t, wa, wb, bt1, wt2, bt2, wt3, y):
    F32, F32R, I32 = mybir.dt.float32, mybir.dt.float32r, mybir.dt.int32
    ALU, ACT, AX = mybir.AluOpType, mybir.ActivationFunctionType, mybir.AxisListType

    ctx = ExitStack()
    with ctx:
        def sb(name, shape, dt=F32):
            return ctx.enter_context(nc.sbuf_tensor(name, shape, dt))

        def ps(name, shape):
            return ctx.enter_context(nc.psum_tensor(name, shape, F32))

        def sem(name):
            return ctx.enter_context(nc.semaphore(name))

        scratch = nc.dram_tensor("embedded", [TILES, SCRATCH_ROWS, COLS], F32, kind="Internal").ap()

        ids_sb = sb("ids_sb", [P, TILES * GATHERS], I32)
        bases_sb = sb("bases_sb", [P, TILES * GATHERS], I32)
        rows_sb = sb("rows_sb", [P, TILES * GATHERS], I32)
        rows_now = sb("rows_now", [P, 2, GATHERS], I32)
        fetched = sb("fetched", [P, 2, GATHERS * DIM])
        unrot = sb("unrot", [P, COLS])
        rot16 = sb("rot16", [P, COLS])
        rot = sb("rot", [P, 2, ROTS, COLS])
        plain = sb("plain", [P, PLAIN_SLOTS, COLS])
        product = sb("product", [P, PRODUCT_SLOTS, COLS])
        part_hi = sb("part_hi", [P, PART_SLOTS, COLS], F32R)
        part_lo = sb("part_lo", [P, PART_SLOTS, COLS], F32R)
        mid_product = sb("mid_product", [P, COLS])
        middle = sb("middle", [P, COLS], F32R)
        hid = sb("hid", [P, 2, 2, COLS])
        w1_sb = sb("w1_sb", [P, CHUNKS1, P])
        w1c_sb = sb("w1c_sb", [P, P])
        w1c_parts = sb("w1c_parts", [P, P], F32R)
        w2_sb = sb("w2_sb", [P, CHUNKS2, P])
        w2_hi = sb("w2_hi", [P, len(SPLIT2), P], F32R)
        w2_lo = sb("w2_lo", [P, len(SPLIT2), P], F32R)
        b1_sb = sb("b1_sb", [P, 1])
        b2_sb = sb("b2_sb", [P, 1])
        za = sb("za", [P, BATCH])
        zb = sb("zb", [P, BATCH])
        wa_sb = sb("wa_sb", [P, TOP1])
        wb_sb = sb("wb_sb", [P, TOP1])
        bt1_sb = sb("bt1_sb", [P, TOP1 // P])
        wt2_sb = sb("wt2_sb", [P, TOP1 // P, TOP2])
        bt2_sb = sb("bt2_sb", [P, TOP2 // P])
        wt3_sb = sb("wt3_sb", [P, TOP2 // P])
        w1b_sb = plain[:, PLAIN_SLOTS - 1, 0:CHUNKS1 * P].rearrange("p (j o) -> p j o", o=P)
        top1 = plain[:, 0:2, :].rearrange("p a c -> p (a c)").rearrange("p (u b) -> p u b", u=TOP1 // P)
        top2 = plain[:, 2, :].rearrange("p (u b) -> p u b", u=TOP2 // P)

        y_sb = plain[0:1, 3, 0:BATCH]

        acc1 = ps("acc1", [P, 2, COLS])
        acc2 = ps("acc2", [P, 2, COLS])

        ids_loaded = sem("ids_loaded")
        rows_ready = sem("rows_ready")
        rows_taken = sem("rows_taken")
        waits_passed = sem("waits_passed")
        fetch_done = [sem(f"fetch_done{i}") for i in range(2)]
        spread_done = [sem(f"spread_done{i}") for i in range(2)]
        rot_a_loaded = [sem(f"rot_a_loaded{i}") for i in range(2)]
        rot_b_loaded = [sem(f"rot_b_loaded{i}") for i in range(2)]
        w1_loaded = sem("w1_loaded")
        w2_loaded = sem("w2_loaded")
        top_loaded = sem("top_loaded")
        w1_ready = sem("w1_ready")
        w1c_rounded = sem("w1c_rounded")
        w2_rounded = sem("w2_rounded")
        w2_ready = sem("w2_ready")
        plain_ready = sem("plain_ready")
        plain_free = sem("plain_free")
        mid_product_ready = sem("mid_product_ready")
        mid_hi_ready = sem("mid_hi_ready")
        middle_ready = sem("middle_ready")
        product_ready = sem("product_ready")
        hi_ready = sem("hi_ready")
        lo_ready = sem("lo_ready")
        parts_free = sem("parts_free")
        acc1_done = sem("acc1_done")
        hid_ready = sem("hid_ready")
        sums1_ready = sem("sums1_ready")
        sums2_ready = sem("sums2_ready")
        top1_done = sem("top1_done")
        top1_ready = sem("top1_ready")
        top2_done = sem("top2_done")
        top2_ready = sem("top2_ready")
        top3_done = sem("top3_done")
        y_ready = sem("y_ready")
        y_stored = sem("y_stored")

        N1, N2 = CHUNKS1, CHUNKS2 - len(SPLIT2)
        S2 = len(SPLIT2)

        def plain_before1(t):
            return 0 if isinstance(t, int) and t == 0 else t * (N1 + N2) - N2

        def plain_before2(t, last=False):
            return t * (N1 + N2) + (1 if last else 2) * N1

        def layer2_plain_upto(c):
            return sum(x not in SPLIT2 for x in range(c + 1))

        def slot_plain1(par, first):
            return 0 if first else (par * (N1 + N2) - N2) % PLAIN_SLOTS

        def slot_plain2(par, last):
            return (par * (N1 + N2) + (1 if last else 2) * N1) % PLAIN_SLOTS

        def chunk_made(eng, t, c, last=False):
            if c in SPLIT2:
                eng.wait_ge(product_ready, S2 * t + SPLIT2.index(c) + 1)
            else:
                eng.wait_ge(plain_ready, plain_before2(t, last) + layer2_plain_upto(c))

        block = ctx.enter_context(nc.Block())

        @block.gpsimd
        def _(pool):
            pool.wait_ge(ids_loaded, 32)
            nc.gpsimd.tensor_tensor(rows_sb[:], ids_sb[:], bases_sb[:], ALU.add).then_inc(rows_ready, 1)
            pool.wait_ge(rows_ready, 1)

            def fetch(t, par, turn):
                if not (isinstance(turn, int) and turn == 0):
                    pool.wait_ge(spread_done[par], 32 * turn)
                    pool.sem_inc(waits_passed, 1)
                nc.gpsimd.tensor_copy(rows_now[:, par, :], rows_sb[:, bass.ds(t * GATHERS, GATHERS)]).then_inc(rows_taken, 1)
                pool.wait_ge(rows_taken, t + 1)
                pool.sem_inc(waits_passed, 1)
                for g in range(GATHERS):
                    nc.gpsimd.indirect_dma_start(
                        out=fetched[:, par, g * DIM:(g + 1) * DIM], out_offset=None, in_=tables,
                        in_offset=bass.IndirectOffsetOnAxis(ap=rows_now[:, par, g:g + 1], axis=0),
                    ).then_inc(fetch_done[par], 16)

            fetch(0, 0, 0)
            fetch(1, 1, 0)
            with pool.Fori(1, TILES // 2) as i:
                for par in range(2):
                    fetch(2 * i + par, par, i)

        @block.sync
        def _(sp):
            sp.dma_start(ids_sb[:], ids).then_inc(ids_loaded, 16)
            sp.dma_start(bases_sb[:], bases).then_inc(ids_loaded, 16)

            def spread(t, par, turn):
                sp.wait_ge(fetch_done[par], 16 * GATHERS * (turn + 1))
                for half in range(2):
                    dst = scratch[bass.ds(t, 1), half * FIELDS:(half + 1) * FIELDS, :]
                    sp.dma_start(dst.rearrange("o m (s c) -> (o m) s c", s=PER_GATHER),
                                 fetched[:, par, :]).then_inc(spread_done[par], 16)

            def rotated(t, first_row, quad_step):
                rows = scratch[bass.ds(t, 1), first_row:first_row + FIELDS, :].rearrange("o m c -> (o m) c")
                return bass.AP(tensor=rows.tensor, offset=rows.offset,
                               ap=[[quad_step * COLS, P // QUAD], [COLS, QUAD], [1, COLS]])

            def load(t, par, turn):
                again = not (isinstance(turn, int) and turn == 0)
                sp.wait_ge(spread_done[par], 32 * (turn + 1))
                if not (isinstance(t, int) and t == 0):
                    sp.wait_ge(plain_ready, plain_before1(t - 1) + N1)
                sp.dma_start(rot16[:], rotated(t, 16, 0)).then_inc(rot_a_loaded[par], 16)
                sp.dma_start(unrot[:], rotated(t, 0, 0)).then_inc(rot_a_loaded[par], 16)
                for j in range(ROTS):
                    if again:
                        chunk_made(sp, t - 2, 2 * j + 1)
                    sp.dma_start(rot[:, par, j, :], rotated(t, 4 * j, 1)).then_inc(
                        (rot_a_loaded if j < CHUNKS1 else rot_b_loaded)[par], 16)

            spread(0, 0, 0)
            load(0, 0, 0)
            spread(1, 1, 0)
            load(1, 1, 0)
            spread(2, 0, 1)
            load(2, 0, 1)
            with sp.Fori(1, TILES // 2 - 1) as i:
                spread(2 * i + 1, 1, i)
                load(2 * i + 1, 1, i)
                spread(2 * i + 2, 0, i + 1)
                load(2 * i + 2, 0, i + 1)
            spread(TILES - 1, 1, TILES // 2 - 1)
            load(TILES - 1, 1, TILES // 2 - 1)
            sp.wait_ge(y_ready, 1)
            sp.dma_start(y, y_sb).then_inc(y_stored, 16)
            sp.wait_ge(y_stored, 16)

        @block.vector
        def _(dve):
            dve.wait_ge(w1_loaded, 64)
            nc.vector.tensor_tensor(w1_sb[:], w1_sb[:], w1b_sb, ALU.add).then_inc(w1_ready, 1)
            dve.wait_ge(w1c_rounded, 1)
            for q in (1, 3):
                at = slice(q * QUAD, (q + 1) * QUAD)
                nc.vector.tensor_tensor(w1c_parts[at, :], w1c_sb[at, :], w1c_parts[at, :].bitcast(F32),
                                        ALU.subtract).then_inc(w1_ready, 1)

            def split_weights():
                for k, c in enumerate(SPLIT2):
                    dve.wait_ge(w2_rounded, k + 1)
                    nc.vector.tensor_tensor(w2_lo[:, k, :], w2_sb[:, c, :], w2_hi[:, k, :].bitcast(F32),
                                            ALU.subtract).then_inc(w2_ready, 1)

            def layer1(t, par, turn, first=False):
                n, n_at = plain_before1(t), slot_plain1(par, first)
                dve.wait_ge(rot_a_loaded[par], 16 * (2 + CHUNKS1) * (turn + 1))
                if not first:
                    dve.wait_ge(middle_ready, t)
                nc.vector.tensor_tensor(mid_product[:], unrot[:], rot16[:],
                                        ALU.mult).then_inc(mid_product_ready, 1)
                for j in range(CHUNKS1):
                    dve.wait_ge(plain_free, n + j + 1)
                    nc.vector.tensor_tensor(plain[:, (n_at + j) % PLAIN_SLOTS, :], unrot[:],
                                            rot[:, par, j, :], ALU.mult).then_inc(plain_ready, 1)
                    if j == CHUNKS1 - 1:
                        dve.wait_ge(mid_hi_ready, t + 1)
                        at = slice(P // 2, P)
                        nc.vector.tensor_tensor(middle[at, :], mid_product[at, :], middle[at, :].bitcast(F32),
                                                ALU.subtract).then_inc(middle_ready, 1)

            def layer2(t, par, turn, last=False):
                n, s = plain_before2(t, last), S2 * t
                n_at, s_at = slot_plain2(par, last), S2 * par
                np_ = 0
                dve.wait_ge(hid_ready, t + 1)
                for c in range(CHUNKS2 + LAG):
                    if c < CHUNKS2:
                        j, arr = c // 2, c % 2
                        if j == CHUNKS1 and arr == 0:
                            dve.wait_ge(rot_b_loaded[par], 16 * (ROTS - CHUNKS1) * (turn + 1))
                        if c in SPLIT2:
                            k = SPLIT2.index(c)
                            if not (isinstance(t, int) and S2 * t + k < PRODUCT_SLOTS):
                                dve.wait_ge(lo_ready, s + k + 1 - PRODUCT_SLOTS)
                            out, ready = product[:, (s_at + k) % PRODUCT_SLOTS, :], product_ready
                        else:
                            dve.wait_ge(plain_free, n + np_ + 1)
                            out, ready = plain[:, (n_at + np_) % PLAIN_SLOTS, :], plain_ready
                            np_ += 1
                        nc.vector.tensor_tensor(out, hid[:, par, arr, :], rot[:, par, j, :],
                                                ALU.mult).then_inc(ready, 1)
                    if c - LAG in SPLIT2:
                        k = SPLIT2.index(c - LAG)
                        dve.wait_ge(hi_ready, s + k + 1)
                        nc.vector.tensor_tensor(part_lo[:, (s_at + k) % PART_SLOTS, :],
                                                product[:, (s_at + k) % PRODUCT_SLOTS, :],
                                                part_hi[:, (s_at + k) % PART_SLOTS, :].bitcast(F32),
                                                ALU.subtract).then_inc(lo_ready, 1)

            layer1(0, 0, 0, first=True)
            split_weights()
            layer1(1, 1, 0)
            layer2(0, 0, 0)
            with dve.Fori(0, TILES // 2 - 1) as i:
                layer1(2 * i + 2, 0, i + 1)
                layer2(2 * i + 1, 1, i)
                layer1(2 * i + 3, 1, i + 1)
                layer2(2 * i + 2, 0, i + 1)
            layer2(TILES - 1, 1, TILES // 2 - 1, last=True)

        @block.scalar
        def _(act):
            act.dma_start(w1_sb[:], w1a).then_inc(w1_loaded, 16)
            act.dma_start(w1b_sb, w1b).then_inc(w1_loaded, 16)
            act.dma_start(w1c_sb[:], w1c).then_inc(w1_loaded, 16)
            act.dma_start(b1_sb[:], b1).then_inc(w1_loaded, 16)
            act.dma_start(w2_sb[:], w2).then_inc(w2_loaded, 16)
            act.dma_start(b2_sb[:], b2).then_inc(w2_loaded, 16)
            act.dma_start(za[0:P // 2, :], dense_t).then_inc(top_loaded, 16)
            act.dma_start(wa_sb[:], wa).then_inc(top_loaded, 16)
            act.dma_start(wb_sb[:], wb).then_inc(top_loaded, 16)
            act.dma_start(bt1_sb[:], bt1).then_inc(top_loaded, 16)
            act.dma_start(wt2_sb[:], wt2).then_inc(top_loaded, 16)
            act.dma_start(bt2_sb[:], bt2).then_inc(top_loaded, 16)
            act.dma_start(wt3_sb[:], wt3).then_inc(top_loaded, 16)

            act.wait_ge(w1_loaded, 64)
            nc.scalar.activation(w1c_parts[:], w1c_sb[:], ACT.Copy).then_inc(w1c_rounded, 1)
            act.wait_ge(w2_loaded, 32)
            for k, c in enumerate(SPLIT2):
                nc.scalar.activation(w2_hi[:, k, :], w2_sb[:, c, :], ACT.Copy).then_inc(w2_rounded, 1)

            def round1(t, first=False):
                act.wait_ge(mid_product_ready, t + 1)
                if not first:
                    act.wait_ge(acc1_done, t)
                nc.scalar.activation(middle[:], mid_product[:], ACT.Copy).then_inc(mid_hi_ready, 1)

            def hidden_rows(t, par, part, fresh=False):
                if part == 0:
                    act.wait_ge(acc1_done, t + 1)
                    if not fresh:
                        chunk_made(act, t - 2, CHUNKS2 - 1)
                    moves = ((0, 0, 64, 0), (0, 64, 64, 0))
                elif part == 1:
                    moves = ((32, 0, 32, 1), (0, 32, 32, 1))
                else:
                    moves = ((32, 64, 32, 1), (0, 96, 32, 1))
                for src, dst, rows, arr in moves:
                    done = nc.scalar.activation(hid[dst:dst + rows, par, arr, :], acc1[src:src + rows, par, :],
                                                ACT.Relu, bias=b1_sb[src:src + rows, :])
                if part == 2:
                    done.then_inc(hid_ready, 1)

            def summed_rows(t, acc, rows, bias, sums, piece):
                for n in range(piece * SAMPLES // 4, (piece + 1) * SAMPLES // 4):
                    at = slice(n * DIM, (n + 1) * DIM)
                    done = nc.scalar.activation(acc[rows, at], acc[rows, at], ACT.Relu, bias=bias[rows, :],
                                                accum_out=sums[rows, bass.ds(t * SAMPLES + n, 1)])
                return done

            def sums1(t, par, piece):
                done = summed_rows(t, acc1[:, par, :], slice(P // 2, P), b1_sb, za, piece)
                if piece == 3:
                    done.then_inc(sums1_ready, 1)

            def sums2(t, par, piece, last=False):
                if piece == 0:
                    act.wait_ge(plain_free, PLAIN_SLOTS + plain_before2(t, last) + N2)
                done = summed_rows(t, acc2[:, par, :], slice(0, P), b2_sb, zb, piece)
                if piece == 3:
                    done.then_inc(sums2_ready, 1)

            def round2(t, par, k):
                n = S2 * t + k
                act.wait_ge(product_ready, n + 1)
                act.wait_ge(parts_free, n + 1)
                nc.scalar.activation(part_hi[:, (S2 * par + k) % PART_SLOTS, :],
                                     product[:, (S2 * par + k) % PRODUCT_SLOTS, :], ACT.Copy).then_inc(hi_ready, 1)

            def step(t, par, first=False, last=False):
                if not last:
                    round1(t + 1)
                for k in range(S2):
                    round2(t, par, k)
                    if not first:
                        for piece in ((), (0, 1), (2, 3))[k] if k < 3 else ():
                            sums2(t - 1, 1 - par, piece)
                    if k >= S2 - 3 and not last:
                        hidden_rows(t + 1, 1 - par, k - (S2 - 3), fresh=first)
                    if k == S2 - 2 and not last:
                        sums1(t + 1, 1 - par, 0)
                if not last:
                    for piece in range(1, 4):
                        sums1(t + 1, 1 - par, piece)

            round1(0, first=True)
            for part in range(3):
                hidden_rows(0, 0, part, fresh=True)
            for piece in range(4):
                sums1(0, 0, piece)
            step(0, 0, first=True)
            with act.Fori(0, TILES // 2 - 1) as i:
                step(2 * i + 1, 1)
                step(2 * i + 2, 0)
            step(TILES - 1, 1, last=True)
            for piece in range(4):
                sums2(TILES - 1, 1, piece, last=True)

            for u in range(TOP1 // P):
                act.wait_ge(top1_done, u + 1)
                if u == 0:
                    act.wait_ge(top_loaded, 112)
                nc.scalar.activation(top1[:, u, :], acc1[:, u // 2, (u % 2) * BANK:(u % 2 + 1) * BANK], ACT.Relu,
                                     bias=bt1_sb[:, u:u + 1]).then_inc(top1_ready, 1)
            for u in range(TOP2 // P):
                act.wait_ge(top2_done, u + 1)
                nc.scalar.activation(top2[:, u, :], acc2[:, 0, u * BANK:(u + 1) * BANK], ACT.Relu,
                                     bias=bt2_sb[:, u:u + 1]).then_inc(top2_ready, 1)
            act.wait_ge(top3_done, 1)
            nc.scalar.activation(y_sb, acc2[0:1, 1, 0:BANK], ACT.Copy).then_inc(y_ready, 1)

        @block.tensor
        def _(pe):
            pe.sem_inc(plain_free, PLAIN_SLOTS)
            pe.sem_inc(parts_free, PART_SLOTS)
            banks = [slice(b * BANK, (b + 1) * BANK) for b in range(COLS // BANK)]

            def layer1(t, par, first=False):
                n, n_at = plain_before1(t), slot_plain1(par, first)
                if not (isinstance(t, int) and t < 2):
                    pe.wait_ge(hid_ready, t - 1)
                    pe.wait_ge(sums1_ready, t - 1)
                for j in range(CHUNKS1):
                    pe.wait_ge(plain_ready, n + j + 1)
                    for at in banks:
                        done = nc.tensor.matmul(acc1[:, par, at], w1_sb[:, j, :],
                                                plain[:, (n_at + j) % PLAIN_SLOTS, at],
                                                start=(j == 0), stop=False)
                    done.then_inc(plain_free, 1)
                pe.wait_ge(middle_ready, t + 1)
                for at in banks:
                    done = nc.tensor.matmul(acc1[:, par, at], w1c_parts[:], middle[:, at], start=False, stop=True)
                done.then_inc(acc1_done, 1)

            def layer2(t, par, last=False):
                n, s = plain_before2(t, last), S2 * t
                n_at, s_at = slot_plain2(par, last), S2 * par
                np_ = 0
                if not (isinstance(t, int) and t < 2):
                    pe.wait_ge(sums2_ready, t - 1)
                for c in range(CHUNKS2):
                    if c in SPLIT2:
                        k = SPLIT2.index(c)
                        slot = (s_at + k) % PART_SLOTS
                        pe.wait_ge(lo_ready, s + k + 1)
                        for w, parts in ((w2_hi, part_hi), (w2_hi, part_lo), (w2_lo, part_hi)):
                            for at in banks:
                                done = nc.tensor.matmul(acc2[:, par, at], w[:, k, :], parts[:, slot, at],
                                                        start=False, stop=False)
                        done.then_inc(parts_free, 1)
                    else:
                        pe.wait_ge(plain_ready, n + np_ + 1)
                        for at in banks:
                            done = nc.tensor.matmul(acc2[:, par, at], w2_sb[:, c, :],
                                                    plain[:, (n_at + np_) % PLAIN_SLOTS, at],
                                                    start=(c == 0), stop=(c == CHUNKS2 - 1))
                        np_ += 1
                        done.then_inc(plain_free, 1)

            pe.wait_ge(w1_ready, 3)
            layer1(0, 0, first=True)
            layer1(1, 1)
            pe.wait_ge(w2_ready, S2)
            layer2(0, 0)
            with pe.Fori(0, TILES // 2 - 1) as i:
                layer1(2 * i + 2, 0)
                layer2(2 * i + 1, 1)
                layer1(2 * i + 3, 1)
                layer2(2 * i + 2, 0)
            layer2(TILES - 1, 1, last=True)

            pe.wait_ge(top_loaded, 112)
            pe.wait_ge(sums1_ready, TILES)
            pe.wait_ge(sums2_ready, TILES)
            for u in range(TOP1 // P):
                at = slice(u * P, (u + 1) * P)
                out = acc1[:, u // 2, (u % 2) * BANK:(u % 2 + 1) * BANK]
                nc.tensor.matmul(out, wa_sb[:, at], za[:], start=True, stop=False)
                nc.tensor.matmul(out, wb_sb[:, at], zb[:], start=False, stop=True).then_inc(top1_done, 1)
            for u in range(TOP1 // P):
                pe.wait_ge(top1_ready, u + 1)
                for v in range(TOP2 // P):
                    done = nc.tensor.matmul(acc2[:, 0, v * BANK:(v + 1) * BANK], wt2_sb[:, u, v * P:(v + 1) * P],
                                            top1[:, u, :], start=(u == 0), stop=(u == TOP1 // P - 1))
                    if u == TOP1 // P - 1:
                        done.then_inc(top2_done, 1)
            for u in range(TOP2 // P):
                pe.wait_ge(top2_ready, u + 1)
                done = nc.tensor.matmul(acc2[0:1, 1, 0:BANK], wt3_sb[:, u:u + 1], top2[:, u, :],
                                        start=(u == 0), stop=(u == TOP2 // P - 1))
            done.then_inc(top3_done, 1)


def kernel(**inputs):
    import numpy as np
    import concourse.bacc as bacc
    from concourse import mybir as mb
    from concourse.bass_utils import run_bass_kernel_spmd as run

    x = {name: np.asarray(a) for name, a in inputs.items()}
    tables = [x[f"tbl_{f}"] for f in range(FIELDS)]
    starts = np.concatenate([[0], np.cumsum([t.shape[0] for t in tables])[:-1]]).astype(np.int32)
    ids = x["ids"].reshape(TILES, PER_GATHER, GATHERS, FIELDS).transpose(3, 1, 0, 2).reshape(P, -1)
    bases = np.broadcast_to(starts[:, None, None], (FIELDS, PER_GATHER, TILES * GATHERS)).reshape(P, -1)

    q, p = np.repeat(np.arange(4), QUAD), np.tile(np.arange(QUAD), 4)
    other = (p[:, None] + 4 * np.arange(ROTS)[None, :] + q[:, None]) % FIELDS
    w1 = x["L0_rec_W1"].reshape(P, FIELDS, FIELDS)
    w1a = w1[:, p[:, None], other[:, :CHUNKS1]].transpose(1, 2, 0)
    w1b = w1[:, other[:, :CHUNKS1], p[:, None]].transpose(1, 2, 0).copy()
    w1b[0:QUAD, 0, :] = 0
    w1c = w1[:, p, (p + 16) % FIELDS].T
    w2 = x["L0_rec_W2"].reshape(P, HIDDEN, FIELDS)
    arr = np.arange(2)[None, None, :]
    hidden = p[:, None, None] + QUAD * ((q[:, None, None] + arr) % 2) + 0 * other[:, :, None]
    w2 = w2[:, hidden, other[:, :, None] + 0 * arr].reshape(P, P, CHUNKS2).transpose(1, 2, 0)

    top = x["W_top1"]
    cin = DIRECT1 + OUT2
    gap = np.zeros((P // 2 - DENSE, TOP1), np.float32)
    dense_t = np.concatenate([x["dense_ctx"].T, np.zeros((P // 2 - DENSE, BATCH), np.float32)])
    laid = {
        "tables": np.concatenate(tables),
        "ids": ids,
        "bases": bases,
        "w1a": w1a,
        "w1b": w1b,
        "w1c": w1c,
        "b1": x["L0_rec_b1"].reshape(P, 1),
        "w2": w2,
        "b2": x["L0_rec_b2"].reshape(P, 1),
        "dense_t": dense_t,
        "wa": np.concatenate([top[cin:], gap, top[:DIRECT1]]),
        "wb": top[DIRECT1:cin],
        "bt1": x["b_top1"].reshape(-1, P).T,
        "wt2": x["W_top2"].reshape(-1, P, TOP2).transpose(1, 0, 2),
        "bt2": x["b_top2"].reshape(-1, P).T,
        "wt3": x["W_top3"].reshape(-1, P).T,
    }
    nc = bacc.Bacc("TRN2", target_bir_lowering=False, num_devices=1)
    arrays, args = {}, []
    for name, a in laid.items():
        a = np.ascontiguousarray(a)
        arrays[f"in_{name}"] = a
        args.append(nc.dram_tensor(f"in_{name}", a.shape, mb.dt.from_np(a.dtype), kind="ExternalInput").ap())
    out = nc.dram_tensor("out_y", (1, BATCH), mb.dt.float32, kind="ExternalOutput").ap()
    cin_tower(nc, *args, out)
    r = run(nc, [arrays], core_ids=[0])
    return r.results[0]["out_y"].reshape(BATCH, 1)
```

```python
import concourse.bass as bass
from concourse import mybir
from contextlib import ExitStack

BATCH, FIELDS, DIM = 512, 32, 64
HIDDEN, DIRECT1, OUT2 = 64, 64, 128
DENSE, TOP1, TOP2 = 16, 512, 256

P = 128
QUAD = 32
BANK = 512
SAMPLES = 16
COLS = SAMPLES * DIM
TILES = BATCH // SAMPLES
PER_GATHER = P // FIELDS
GATHERS = SAMPLES // PER_GATHER
ROTS = FIELDS * HIDDEN // P // 2
CHUNKS1 = 4
CHUNKS2 = 2 * ROTS
SCRATCH_ROWS = 2 * FIELDS

SPLIT2 = (1, 2, 3, 4, 6, 7, 8, 9, 11, 12, 13, 14)
BY_POOL = (1, 2, 4, 6, 7, 8, 11, 12, 13, 14)
LAG = 2
PLAIN1_SLOTS = CHUNKS1
PLAIN2_SLOTS = 2
PRODUCT_SLOTS = 6
PART_SLOTS = 6
LAYER1_AFTER = {10: CHUNKS1, 11: 0, 12: 1, 13: 2, 15: 3}
MIDDLE_LOW_AFTER = 13
HIDDEN_AFTER = 8
SUMS2_AFTER = (3, 3, 4, 4)
SUMS1_AFTER = (9, 11, 13, 14)
ROUND1_AFTER = 12
assert HIDDEN_AFTER in SPLIT2 and ROUND1_AFTER in SPLIT2
assert (2 * (CHUNKS2 - len(SPLIT2))) % PLAIN2_SLOTS == 0
assert (2 * len(SPLIT2)) % PART_SLOTS == 0 and (2 * len(SPLIT2)) % PRODUCT_SLOTS == 0
assert CHUNKS2 - 1 not in SPLIT2


def cin_tower(nc, tables, ids, bases, w1a, w1b, w1c, b1, w2, b2, dense_t, wa, wb, bt1, wt2, bt2, wt3, y):
    F32, F32R, I32 = mybir.dt.float32, mybir.dt.float32r, mybir.dt.int32
    ALU, ACT, AX = mybir.AluOpType, mybir.ActivationFunctionType, mybir.AxisListType

    ctx = ExitStack()
    with ctx:
        def sb(name, shape, dt=F32):
            return ctx.enter_context(nc.sbuf_tensor(name, shape, dt))

        def ps(name, shape):
            return ctx.enter_context(nc.psum_tensor(name, shape, F32))

        def sem(name):
            return ctx.enter_context(nc.semaphore(name))

        scratch = nc.dram_tensor("embedded", [TILES, SCRATCH_ROWS, COLS], F32, kind="Internal").ap()

        ids_sb = sb("ids_sb", [P, TILES * GATHERS], I32)
        bases_sb = sb("bases_sb", [P, TILES * GATHERS], I32)
        rows_sb = sb("rows_sb", [P, TILES * GATHERS], I32)
        rows_now = sb("rows_now", [P, 2, GATHERS], I32)
        fetched = sb("fetched", [P, 2, GATHERS * DIM])
        unrot = sb("unrot", [P, COLS])
        rot16 = sb("rot16", [P, COLS])
        rot = sb("rot", [P, 2, ROTS, COLS])
        plain1 = sb("plain1", [P, PLAIN1_SLOTS, COLS])
        plain2 = sb("plain2", [P, PLAIN2_SLOTS, COLS])
        product = sb("product", [P, PRODUCT_SLOTS, COLS])
        part_hi = sb("part_hi", [P, PART_SLOTS, COLS], F32R)
        part_lo = sb("part_lo", [P, PART_SLOTS, COLS], F32R)
        mid_product = sb("mid_product", [P, COLS])
        middle = sb("middle", [P, COLS], F32R)
        w1_sb = sb("w1_sb", [P, CHUNKS1, P])
        w1c_sb = sb("w1c_sb", [P, P])
        w1c_parts = sb("w1c_parts", [P, P], F32R)
        w2_sb = sb("w2_sb", [P, CHUNKS2, P])
        w2_hi = sb("w2_hi", [P, len(SPLIT2), P], F32R)
        w2_lo = sb("w2_lo", [P, len(SPLIT2), P], F32R)
        b1_sb = sb("b1_sb", [P, 1])
        b2_sb = sb("b2_sb", [P, 1])
        za = sb("za", [P, BATCH])
        zb = sb("zb", [P, BATCH])
        bt1_sb = sb("bt1_sb", [P, TOP1 // P])
        bt2_sb = sb("bt2_sb", [P, TOP2 // P])
        wt3_sb = sb("wt3_sb", [P, TOP2 // P])
        w1b_sb = product[:, PRODUCT_SLOTS - 1, 0:CHUNKS1 * P].rearrange("p (j o) -> p j o", o=P)
        wa_sb = rot[:, 0, 0, 0:TOP1]
        wb_sb = rot[:, 0, 0, TOP1:2 * TOP1]
        wt2_sb = rot[:, 0, 1, :].rearrange("p (u v) -> p u v", v=TOP2)
        top1 = plain1[:, 0:2, :].rearrange("p a c -> p (a c)").rearrange("p (u b) -> p u b", u=TOP1 // P)
        top2 = plain1[:, 2, :].rearrange("p (u b) -> p u b", u=TOP2 // P)

        y_sb = plain1[0:1, 3, 0:BATCH]

        acc1 = ps("acc1", [P, COLS])
        acc2 = ps("acc2", [P, COLS])
        hid = ps("hid", [P, 2, COLS])

        top1_acc = hid[:].rearrange("p a (u b) -> p (a u) b", b=BANK)

        ids_loaded = sem("ids_loaded")
        rows_ready = sem("rows_ready")
        rows_taken = sem("rows_taken")
        waits_passed = sem("waits_passed")
        fetch_done = [sem(f"fetch_done{i}") for i in range(2)]
        spread_done = [sem(f"spread_done{i}") for i in range(2)]
        rot_a_loaded = [[sem(f"rot_a_loaded{i}_{j}") for j in range(CHUNKS1 + 1)] for i in range(2)]
        rot_b_loaded = [sem(f"rot_b_loaded{i}") for i in range(2)]
        w1_loaded = sem("w1_loaded")
        w2_loaded = sem("w2_loaded")
        top_loaded = sem("top_loaded")
        w1_ready = sem("w1_ready")
        w1c_rounded = sem("w1c_rounded")
        w2_rounded = sem("w2_rounded")
        w2_ready = sem("w2_ready")
        plain1_ready = sem("plain1_ready")
        plain1_free = sem("plain1_free")
        plain2_ready = sem("plain2_ready")
        plain2_free = sem("plain2_free")
        mid_product_ready = sem("mid_product_ready")
        mid_hi_ready = sem("mid_hi_ready")
        middle_ready = sem("middle_ready")
        product_ready = sem("product_ready")
        hi_ready = sem("hi_ready")
        lo_by_vector = sem("lo_by_vector")
        lo_by_pool = sem("lo_by_pool")
        parts_free = sem("parts_free")
        acc1_done = sem("acc1_done")
        hid_ready = [sem(f"hid_ready{a}") for a in range(2)]
        sums1_ready = sem("sums1_ready")
        sums2_ready = sem("sums2_ready")
        top1_done = sem("top1_done")
        top1_ready = sem("top1_ready")
        top2_done = sem("top2_done")
        top2_ready = sem("top2_ready")
        top3_done = sem("top3_done")
        y_ready = sem("y_ready")
        y_stored = sem("y_stored")

        N1, N2 = CHUNKS1, CHUNKS2 - len(SPLIT2)
        S2 = len(SPLIT2)

        def layer2_plain_upto(c):
            return sum(x not in SPLIT2 for x in range(c + 1))

        SP2 = len(BY_POOL)

        def parts_made(eng, t, k, before=0):
            t, k = (t, k - before) if k >= before else (t - 1, k - before + S2)
            c = SPLIT2[k]
            if c in BY_POOL:
                eng.wait_ge(lo_by_pool, SP2 * t + BY_POOL.index(c) + 1)
            else:
                eng.wait_ge(lo_by_vector, (S2 - SP2) * t + [x for x in SPLIT2 if x not in BY_POOL].index(c) + 1)

        def chunk_made(eng, t, c):
            if c in SPLIT2:
                eng.wait_ge(product_ready, S2 * t + SPLIT2.index(c) + 1)
            else:
                eng.wait_ge(plain2_ready, N2 * t + layer2_plain_upto(c))

        block = ctx.enter_context(nc.Block())

        @block.gpsimd
        def _(pool):
            pool.wait_ge(ids_loaded, 32)
            nc.gpsimd.tensor_tensor(rows_sb[:], ids_sb[:], bases_sb[:], ALU.add).then_inc(rows_ready, 1)
            pool.wait_ge(rows_ready, 1)

            def rows_of(t, par, turn):
                if not (isinstance(turn, int) and turn == 0):
                    pool.wait_ge(spread_done[par], 32 * turn)
                    pool.sem_inc(waits_passed, 1)
                nc.gpsimd.tensor_copy(rows_now[:, par, :], rows_sb[:, bass.ds(t * GATHERS, GATHERS)]).then_inc(rows_taken, 1)
                pool.wait_ge(rows_taken, t + 1)
                pool.sem_inc(waits_passed, 1)

            def fetch(par, g):
                nc.gpsimd.indirect_dma_start(
                    out=fetched[:, par, g * DIM:(g + 1) * DIM], out_offset=None, in_=tables,
                    in_offset=bass.IndirectOffsetOnAxis(ap=rows_now[:, par, g:g + 1], axis=0),
                ).then_inc(fetch_done[par], 16)

            def step(t, par, turn, fetching=True):
                if fetching:
                    rows_of(t + 3, 1 - par, turn)
                for n, c in enumerate(BY_POOL):
                    k = SPLIT2.index(c)
                    pool.wait_ge(hi_ready, S2 * t + k + 1)
                    nc.gpsimd.tensor_tensor(part_lo[:, (S2 * par + k) % PART_SLOTS, :],
                                            product[:, (S2 * par + k) % PRODUCT_SLOTS, :],
                                            part_hi[:, (S2 * par + k) % PART_SLOTS, :].bitcast(F32),
                                            ALU.subtract).then_inc(lo_by_pool, 1)
                    if fetching and n % 2 == 1 and n // 2 < GATHERS:
                        fetch(1 - par, n // 2)

            for t in range(3):
                rows_of(t, t % 2, t // 2)
                for g in range(GATHERS):
                    fetch(t % 2, g)
            step(0, 0, 1)
            with pool.Fori(0, (TILES - 4) // 2) as i:
                step(2 * i + 1, 1, i + 2)
                step(2 * i + 2, 0, i + 2)
            for t in range(TILES - 3, TILES):
                step(t, t % 2, None, fetching=False)

        @block.sync
        def _(sp):
            sp.dma_start(ids_sb[:], ids).then_inc(ids_loaded, 16)

            def spread(t, par, turn):
                sp.wait_ge(fetch_done[par], 16 * GATHERS * (turn + 1))
                for half in range(2):
                    dst = scratch[bass.ds(t, 1), half * FIELDS:(half + 1) * FIELDS, :]
                    sp.dma_start(dst.rearrange("o m (s c) -> (o m) s c", s=PER_GATHER),
                                 fetched[:, par, :]).then_inc(spread_done[par], 16)

            def rotated(t, first_row, quad_step):
                rows = scratch[bass.ds(t, 1), first_row:first_row + FIELDS, :].rearrange("o m c -> (o m) c")
                return bass.AP(tensor=rows.tensor, offset=rows.offset,
                               ap=[[quad_step * COLS, P // QUAD], [COLS, QUAD], [1, COLS]])

            def load1(t, par, turn):
                sp.wait_ge(spread_done[par], 32 * (turn + 1))
                sp.sem_inc(waits_passed, 1)
                if not (isinstance(t, int) and t == 0):
                    sp.wait_ge(plain1_ready, N1 * t)
                    sp.sem_inc(waits_passed, 1)
                    sp.wait_ge(mid_product_ready, t)
                sp.dma_start(unrot[:], rotated(t, 0, 0)).then_inc(rot_a_loaded[par][CHUNKS1], 16)
                sp.dma_start(rot16[:], rotated(t, 16, 0)).then_inc(rot_a_loaded[par][CHUNKS1], 16)
                for j in range(CHUNKS1):
                    if not (isinstance(t, int) and t < 2):
                        chunk_made(sp, t - 2, ROTS + j)
                    sp.dma_start(rot[:, par, j, :], rotated(t, 4 * j, 1)).then_inc(rot_a_loaded[par][j], 16)

            def load2(t, par):
                for j in range(CHUNKS1, ROTS):
                    if not (isinstance(t, int) and t < 2):
                        chunk_made(sp, t - 2, ROTS + j)
                    sp.dma_start(rot[:, par, j, :], rotated(t, 4 * j, 1)).then_inc(rot_b_loaded[par], 16)

            def load(t, par, turn):
                spread(t, par, turn)
                load1(t, par, turn)
                load2(t, par)

            spread(0, 0, 0)
            load1(0, 0, 0)
            spread(1, 1, 0)
            load1(1, 1, 0)
            load2(0, 0)
            load2(1, 1)
            load(2, 0, 1)
            with sp.Fori(1, TILES // 2 - 1) as i:
                load(2 * i + 1, 1, i)
                load(2 * i + 2, 0, i + 1)
            load(TILES - 1, 1, TILES // 2 - 1)
            sp.wait_ge(y_ready, 1)
            sp.dma_start(y, y_sb).then_inc(y_stored, 16)
            sp.wait_ge(y_stored, 16)

        @block.vector
        def _(dve):
            dve.wait_ge(w1_loaded, 64)
            nc.vector.tensor_tensor(w1_sb[:], w1_sb[:], w1b_sb, ALU.add).then_inc(w1_ready, 1)
            dve.wait_ge(w1c_rounded, 1)
            for q in (1, 3):
                at = slice(q * QUAD, (q + 1) * QUAD)
                nc.vector.tensor_tensor(w1c_parts[at, :], w1c_sb[at, :], w1c_parts[at, :].bitcast(F32),
                                        ALU.subtract).then_inc(w1_ready, 1)

            def split_weights():
                for k, c in enumerate(SPLIT2):
                    dve.wait_ge(w2_rounded, k + 1)
                    nc.vector.tensor_tensor(w2_lo[:, k, :], w2_sb[:, c, :], w2_hi[:, k, :].bitcast(F32),
                                            ALU.subtract).then_inc(w2_ready, 1)

            def layer1(t, par, turn, j, first=False):
                if j == CHUNKS1:
                    dve.wait_ge(rot_a_loaded[par][j], 32 * (turn + 1))
                    if not first:
                        dve.wait_ge(middle_ready, t)
                    nc.vector.tensor_tensor(mid_product[:], unrot[:], rot16[:],
                                            ALU.mult).then_inc(mid_product_ready, 1)
                else:
                    dve.wait_ge(rot_a_loaded[par][j], 16 * (turn + 1))
                    if not first:
                        dve.wait_ge(plain1_free, N1 * (t - 1) + j + 1)
                    nc.vector.tensor_tensor(plain1[:, j, :], unrot[:], rot[:, par, j, :],
                                            ALU.mult).then_inc(plain1_ready, 1)

            def middle_low(t):
                dve.wait_ge(mid_hi_ready, t + 1)
                at = slice(P // 2, P)
                nc.vector.tensor_tensor(middle[at, :], mid_product[at, :], middle[at, :].bitcast(F32),
                                        ALU.subtract).then_inc(middle_ready, 1)

            def step(t, par, turn, layer1_too=True):
                s, s_at, n_at = S2 * t, S2 * par, N2 * par
                np_ = 0
                for c in range(CHUNKS2 + LAG):
                    if c < CHUNKS2:
                        arr, j = c // ROTS, c % ROTS
                        if j == 0:
                            dve.wait_ge(hid_ready[arr], t + 1)
                        if c == CHUNKS1:
                            dve.wait_ge(rot_b_loaded[par], 16 * (ROTS - CHUNKS1) * (turn + 1))
                        if c in SPLIT2:
                            k = SPLIT2.index(c)
                            if not (isinstance(t, int) and S2 * t + k < PRODUCT_SLOTS):
                                parts_made(dve, t, k, before=PRODUCT_SLOTS)
                            out, ready = product[:, (s_at + k) % PRODUCT_SLOTS, :], product_ready
                        else:
                            dve.wait_ge(plain2_free, N2 * t + np_ + 1)
                            out, ready = plain2[:, (n_at + np_) % PLAIN2_SLOTS, :], plain2_ready
                            np_ += 1
                        nc.vector.tensor_tensor(out, hid[:, arr, :], rot[:, par, j, :],
                                                ALU.mult).then_inc(ready, 1)
                    if c in LAYER1_AFTER and layer1_too:
                        layer1(t + 2, par, turn + 1, LAYER1_AFTER[c])
                    if c == MIDDLE_LOW_AFTER and layer1_too:
                        middle_low(t + 2)
                    if c - LAG in SPLIT2 and c - LAG not in BY_POOL:
                        k = SPLIT2.index(c - LAG)
                        dve.wait_ge(hi_ready, s + k + 1)
                        nc.vector.tensor_tensor(part_lo[:, (s_at + k) % PART_SLOTS, :],
                                                product[:, (s_at + k) % PRODUCT_SLOTS, :],
                                                part_hi[:, (s_at + k) % PART_SLOTS, :].bitcast(F32),
                                                ALU.subtract).then_inc(lo_by_vector, 1)

            for t in range(2):
                for j in (CHUNKS1, *range(CHUNKS1)):
                    layer1(t, t, 0, j, first=(t == 0))
                middle_low(t)
            split_weights()
            step(0, 0, 0)
            with dve.Fori(0, (TILES - 4) // 2) as i:
                step(2 * i + 1, 1, i)
                step(2 * i + 2, 0, i + 1)
            for t in range(TILES - 3, TILES):
                step(t, t % 2, t // 2, layer1_too=(t + 2 < TILES))

        @block.scalar
        def _(act):
            act.dma_start(bases_sb[:], bases).then_inc(ids_loaded, 16)
            act.dma_start(w1_sb[:], w1a).then_inc(w1_loaded, 16)
            act.dma_start(w1b_sb, w1b).then_inc(w1_loaded, 16)
            act.dma_start(w1c_sb[:], w1c).then_inc(w1_loaded, 16)
            act.dma_start(b1_sb[:], b1).then_inc(w1_loaded, 16)
            act.wait_ge(w1_loaded, 64)
            nc.scalar.activation(w1c_parts[:], w1c_sb[:], ACT.Copy).then_inc(w1c_rounded, 1)
            def round1(t, first=False):
                act.wait_ge(mid_product_ready, t + 1)
                if not first:
                    act.wait_ge(acc1_done, t)
                nc.scalar.activation(middle[:], mid_product[:], ACT.Copy).then_inc(mid_hi_ready, 1)

            def hidden_rows(t, part, fresh=False, last=False):
                if part == 0:
                    act.wait_ge(acc1_done, t + 1)
                if part < 2 and not fresh:
                    chunk_made(act, t - 1, (ROTS - 1, CHUNKS2 - 1)[part])
                if part == 0:
                    moves = ((0, 0, 64, 0), (0, 64, 64, 0))
                elif part == 1:
                    moves = ((32, 0, 32, 1), (0, 32, 32, 1))
                else:
                    moves = ((32, 64, 32, 1), (0, 96, 32, 1))
                for src, dst, rows, arr in moves:
                    done = nc.scalar.activation(hid[dst:dst + rows, arr, :], acc1[src:src + rows, :],
                                                ACT.Relu, bias=b1_sb[src:src + rows, :])
                if part != 1:
                    done.then_inc(hid_ready[part // 2], 1)

            def summed_rows(t, acc, rows, bias, sums, piece):
                for n in range(piece * SAMPLES // 4, (piece + 1) * SAMPLES // 4):
                    at = slice(n * DIM, (n + 1) * DIM)
                    done = nc.scalar.activation(acc[rows, at], acc[rows, at], ACT.Relu, bias=bias[rows, :],
                                                accum_out=sums[rows, bass.ds(t * SAMPLES + n, 1)])
                return done

            def sums1(t, piece):
                done = summed_rows(t, acc1[:], slice(P // 2, P), b1_sb, za, piece)
                if piece == 3:
                    done.then_inc(sums1_ready, 1)

            def sums2(t, piece):
                if piece == 0:
                    act.wait_ge(plain2_free, PLAIN2_SLOTS + N2 * (t + 1))
                done = summed_rows(t, acc2[:], slice(0, P), b2_sb, zb, piece)
                if piece == 3:
                    done.then_inc(sums2_ready, 1)

            def round2(t, par, k):
                n = S2 * t + k
                act.wait_ge(product_ready, n + 1)
                act.wait_ge(parts_free, n + 1)
                nc.scalar.activation(part_hi[:, (S2 * par + k) % PART_SLOTS, :],
                                     product[:, (S2 * par + k) % PRODUCT_SLOTS, :], ACT.Copy).then_inc(hi_ready, 1)

            def step(t, par, first=False, ahead=2):
                if not first:
                    hidden_rows(t, 1)
                    hidden_rows(t, 2)
                if ahead == 0:
                    act.dma_start(wa_sb, wa).then_inc(top_loaded, 16)
                    act.dma_start(wb_sb, wb).then_inc(top_loaded, 16)
                    act.dma_start(wt2_sb, wt2).then_inc(top_loaded, 16)
                for k, c in enumerate(SPLIT2):
                    round2(t, par, k)
                    for piece in range(4):
                        if not first and c == SUMS2_AFTER[piece]:
                            sums2(t - 1, piece)
                        if ahead > 0 and c == SUMS1_AFTER[piece]:
                            sums1(t + 1, piece)
                    if ahead > 0 and c == HIDDEN_AFTER:
                        hidden_rows(t + 1, 0)
                    if ahead > 1 and c == ROUND1_AFTER:
                        round1(t + 2)

            round1(0, first=True)
            act.dma_start(w2_sb[:], w2).then_inc(w2_loaded, 16)
            act.dma_start(b2_sb[:], b2).then_inc(w2_loaded, 16)
            hidden_rows(0, 0, fresh=True)
            hidden_rows(0, 1, fresh=True)
            hidden_rows(0, 2)
            for piece in range(4):
                sums1(0, piece)
            round1(1)
            act.wait_ge(w2_loaded, 32)
            for k, c in enumerate(SPLIT2):
                nc.scalar.activation(w2_hi[:, k, :], w2_sb[:, c, :], ACT.Copy).then_inc(w2_rounded, 1)
            step(0, 0, first=True)
            act.dma_start(za[0:P // 2, :], dense_t).then_inc(top_loaded, 16)
            act.dma_start(bt1_sb[:], bt1).then_inc(top_loaded, 16)
            act.dma_start(bt2_sb[:], bt2).then_inc(top_loaded, 16)
            act.dma_start(wt3_sb[:], wt3).then_inc(top_loaded, 16)
            with act.Fori(0, (TILES - 4) // 2) as i:
                step(2 * i + 1, 1)
                step(2 * i + 2, 0)
            for t in range(TILES - 3, TILES):
                step(t, t % 2, ahead=TILES - 1 - t)
            for piece in range(4):
                sums2(TILES - 1, piece)

            for u in range(TOP1 // P):
                act.wait_ge(top1_done, u + 1)
                if u == 0:
                    act.wait_ge(top_loaded, 112)
                nc.scalar.activation(top1[:, u, :], top1_acc[:, u, :], ACT.Relu,
                                     bias=bt1_sb[:, u:u + 1]).then_inc(top1_ready, 1)
            for u in range(TOP2 // P):
                act.wait_ge(top2_done, u + 1)
                nc.scalar.activation(top2[:, u, :], acc2[:, u * BANK:(u + 1) * BANK], ACT.Relu,
                                     bias=bt2_sb[:, u:u + 1]).then_inc(top2_ready, 1)
            act.wait_ge(top3_done, 1)
            nc.scalar.activation(y_sb, acc1[0:1, 0:BANK], ACT.Copy).then_inc(y_ready, 1)

        @block.tensor
        def _(pe):
            pe.sem_inc(plain2_free, PLAIN2_SLOTS)
            pe.sem_inc(parts_free, PART_SLOTS)
            banks = [slice(b * BANK, (b + 1) * BANK) for b in range(COLS // BANK)]

            def layer1(t, first=False):
                if not first:
                    pe.wait_ge(hid_ready[1], t)
                    pe.wait_ge(sums1_ready, t)
                for j in range(CHUNKS1):
                    pe.wait_ge(plain1_ready, N1 * t + j + 1)
                    for at in banks:
                        done = nc.tensor.matmul(acc1[:, at], w1_sb[:, j, :], plain1[:, j, at],
                                                start=(j == 0), stop=False)
                    done.then_inc(plain1_free, 1)
                pe.wait_ge(middle_ready, t + 1)
                for at in banks:
                    done = nc.tensor.matmul(acc1[:, at], w1c_parts[:], middle[:, at], start=False, stop=True)
                done.then_inc(acc1_done, 1)

            def layer2(t, par):
                n, n_at, s_at = N2 * t, N2 * par, S2 * par
                np_ = 0
                if not (isinstance(t, int) and t == 0):
                    pe.wait_ge(sums2_ready, t)
                for c in range(CHUNKS2):
                    if c in SPLIT2:
                        k = SPLIT2.index(c)
                        slot = (s_at + k) % PART_SLOTS
                        parts_made(pe, t, k)
                        for w, parts in ((w2_hi, part_hi), (w2_hi, part_lo), (w2_lo, part_hi)):
                            for at in banks:
                                done = nc.tensor.matmul(acc2[:, at], w[:, k, :], parts[:, slot, at],
                                                        start=False, stop=False)
                        done.then_inc(parts_free, 1)
                    else:
                        pe.wait_ge(plain2_ready, n + np_ + 1)
                        for at in banks:
                            done = nc.tensor.matmul(acc2[:, at], w2_sb[:, c, :],
                                                    plain2[:, (n_at + np_) % PLAIN2_SLOTS, at],
                                                    start=(c == 0), stop=(c == CHUNKS2 - 1))
                        np_ += 1
                        done.then_inc(plain2_free, 1)

            pe.wait_ge(w1_ready, 3)
            layer1(0, first=True)
            layer1(1)
            pe.wait_ge(w2_ready, S2)
            layer2(0, 0)
            with pe.Fori(0, TILES // 2 - 1) as i:
                layer1(2 * i + 2)
                layer2(2 * i + 1, 1)
                layer1(2 * i + 3)
                layer2(2 * i + 2, 0)
            layer2(TILES - 1, 1)

            pe.wait_ge(top_loaded, 112)
            pe.wait_ge(sums1_ready, TILES)
            chunk_made(pe, TILES - 1, CHUNKS2 - 1)
            for u in range(TOP1 // P):
                nc.tensor.matmul(top1_acc[:, u, :], wa_sb[:, u * P:(u + 1) * P], za[:], start=True, stop=False)
            pe.wait_ge(sums2_ready, TILES)
            for u in range(TOP1 // P):
                nc.tensor.matmul(top1_acc[:, u, :], wb_sb[:, u * P:(u + 1) * P], zb[:], start=False,
                                 stop=True).then_inc(top1_done, 1)
            for u in range(TOP1 // P):
                pe.wait_ge(top1_ready, u + 1)
                for v in range(TOP2 // P):
                    done = nc.tensor.matmul(acc2[:, v * BANK:(v + 1) * BANK], wt2_sb[:, u, v * P:(v + 1) * P],
                                            top1[:, u, :], start=(u == 0), stop=(u == TOP1 // P - 1))
                    if u == TOP1 // P - 1:
                        done.then_inc(top2_done, 1)
            for u in range(TOP2 // P):
                pe.wait_ge(top2_ready, u + 1)
                done = nc.tensor.matmul(acc1[0:1, 0:BANK], wt3_sb[:, u:u + 1], top2[:, u, :],
                                        start=(u == 0), stop=(u == TOP2 // P - 1))
            done.then_inc(top3_done, 1)


def kernel(**inputs):
    import numpy as np
    import concourse.bacc as bacc
    from concourse import mybir as mb
    from concourse.bass_utils import run_bass_kernel_spmd as run

    x = {name: np.asarray(a) for name, a in inputs.items()}
    tables = [x[f"tbl_{f}"] for f in range(FIELDS)]
    starts = np.concatenate([[0], np.cumsum([t.shape[0] for t in tables])[:-1]]).astype(np.int32)
    ids = x["ids"].reshape(TILES, PER_GATHER, GATHERS, FIELDS).transpose(3, 1, 0, 2).reshape(P, -1)
    bases = np.broadcast_to(starts[:, None, None], (FIELDS, PER_GATHER, TILES * GATHERS)).reshape(P, -1)

    q, p = np.repeat(np.arange(4), QUAD), np.tile(np.arange(QUAD), 4)
    other = (p[:, None] + 4 * np.arange(ROTS)[None, :] + q[:, None]) % FIELDS
    w1 = x["L0_rec_W1"].reshape(P, FIELDS, FIELDS)
    w1a = w1[:, p[:, None], other[:, :CHUNKS1]].transpose(1, 2, 0)
    w1b = w1[:, other[:, :CHUNKS1], p[:, None]].transpose(1, 2, 0).copy()
    w1b[0:QUAD, 0, :] = 0
    w1c = w1[:, p, (p + 16) % FIELDS].T
    w2 = x["L0_rec_W2"].reshape(P, HIDDEN, FIELDS)
    arr = np.arange(2)[None, :, None]
    hidden = p[:, None, None] + QUAD * ((q[:, None, None] + arr) % 2) + 0 * other[:, None, :]
    w2 = w2[:, hidden, other[:, None, :] + 0 * arr].reshape(P, P, CHUNKS2).transpose(1, 2, 0)

    top = x["W_top1"]
    cin = DIRECT1 + OUT2
    gap = np.zeros((P // 2 - DENSE, TOP1), np.float32)
    dense_t = np.concatenate([x["dense_ctx"].T, np.zeros((P // 2 - DENSE, BATCH), np.float32)])
    laid = {
        "tables": np.concatenate(tables),
        "ids": ids,
        "bases": bases,
        "w1a": w1a,
        "w1b": w1b,
        "w1c": w1c,
        "b1": x["L0_rec_b1"].reshape(P, 1),
        "w2": w2,
        "b2": x["L0_rec_b2"].reshape(P, 1),
        "dense_t": dense_t,
        "wa": np.concatenate([top[cin:], gap, top[:DIRECT1]]),
        "wb": top[DIRECT1:cin],
        "bt1": x["b_top1"].reshape(-1, P).T,
        "wt2": x["W_top2"].reshape(-1, P, TOP2).transpose(1, 0, 2),
        "bt2": x["b_top2"].reshape(-1, P).T,
        "wt3": x["W_top3"].reshape(-1, P).T,
    }
    nc = bacc.Bacc("TRN2", target_bir_lowering=False, num_devices=1)
    arrays, args = {}, []
    for name, a in laid.items():
        a = np.ascontiguousarray(a)
        arrays[f"in_{name}"] = a
        args.append(nc.dram_tensor(f"in_{name}", a.shape, mb.dt.from_np(a.dtype), kind="ExternalInput").ap())
    out = nc.dram_tensor("out_y", (1, BATCH), mb.dt.float32, kind="ExternalOutput").ap()
    cin_tower(nc, *args, out)
    r = run(nc, [arrays], core_ids=[0])
    return r.results[0]["out_y"].reshape(BATCH, 1)
```

```python
import concourse.bass as bass
from concourse import mybir
from contextlib import ExitStack

BATCH, FIELDS, DIM = 512, 32, 64
HIDDEN, DIRECT1, OUT2 = 64, 64, 128
DENSE, TOP1, TOP2 = 16, 512, 256

P = 128
QUAD = 32
BANK = 512
SAMPLES = 16
COLS = SAMPLES * DIM
TILES = BATCH // SAMPLES
PER_GATHER = P // FIELDS
GATHERS = SAMPLES // PER_GATHER
ROTS = FIELDS * HIDDEN // P // 2
CHUNKS1 = 4
CHUNKS2 = 2 * ROTS
SCRATCH_ROWS = 2 * FIELDS

SPLIT2 = (1, 2, 3, 4, 6, 7, 8, 9, 11, 12, 13, 14)
VECTOR_LOW_AFTER = {2: 4, 7: 9, 11: 14}
LAST_VECTOR_LOW_AFTER = {2: 4, 7: 9, 11: 13, 14: 15}
PLAIN1_SLOTS = CHUNKS1
PLAIN2_SLOTS = 2
PRODUCT_SLOTS = 6
PART_SLOTS = 6
LAYER1_AFTER = {10: CHUNKS1, 11: 0, 12: 1, 13: 2, 15: 3}
MIDDLE_LOW_AFTER = 15
HIDDEN_AFTER = 8
SUMS1_AFTER = (11, 12, 14, 14)
SUMS2_AFTER = (3, 4, 4, 4)
ROUND1_AFTER = 12
FETCH_AFTER = (1, 3, 5, 7)
START_LAYER1_AFTER = {3: CHUNKS1, 4: 0, 5: 1, 6: 2, 7: 3}
START_MIDDLE_LOW_AFTER = 6
START_ROUND1_AFTER = 4
START_SWAPPED_AFTER = (1, 2)
START_SUMS1_AFTER = (3, 3, 4, 4)
START_CHUNKS = 5
TOP_AFTER_CHUNKS = 9
assert HIDDEN_AFTER in SPLIT2 and ROUND1_AFTER in SPLIT2
assert (2 * (CHUNKS2 - len(SPLIT2))) % PLAIN2_SLOTS == 0
assert (2 * len(SPLIT2)) % PART_SLOTS == 0 and (2 * len(SPLIT2)) % PRODUCT_SLOTS == 0
assert CHUNKS2 - 1 not in SPLIT2


def cin_tower(nc, tables, ids, bases, w1a, w1b, w1c, b1, w2, b2, dense_t, wa, wb, bt1, wt2, bt2, wt3, y):
    F32, F32R, I32 = mybir.dt.float32, mybir.dt.float32r, mybir.dt.int32
    ALU, ACT, AX = mybir.AluOpType, mybir.ActivationFunctionType, mybir.AxisListType

    ctx = ExitStack()
    with ctx:
        def sb(name, shape, dt=F32):
            return ctx.enter_context(nc.sbuf_tensor(name, shape, dt))

        def ps(name, shape):
            return ctx.enter_context(nc.psum_tensor(name, shape, F32))

        def sem(name):
            return ctx.enter_context(nc.semaphore(name))

        scratch = nc.dram_tensor("embedded", [TILES, SCRATCH_ROWS, COLS], F32, kind="Internal").ap()

        ids_sb = sb("ids_sb", [P, TILES * GATHERS], I32)
        rows_sb = sb("rows_sb", [P, TILES * GATHERS], I32)
        rows_now = sb("rows_now", [P, 2, GATHERS], I32)
        fetched = sb("fetched", [P, 2, GATHERS * DIM])
        unrot = sb("unrot", [P, COLS])
        rot16 = sb("rot16", [P, COLS])
        rot = sb("rot", [P, 2, ROTS, COLS])
        plain1 = sb("plain1", [P, PLAIN1_SLOTS, COLS])
        plain2 = sb("plain2", [P, PLAIN2_SLOTS, COLS])
        product = sb("product", [P, PRODUCT_SLOTS, COLS])
        part_hi = sb("part_hi", [P, PART_SLOTS, COLS], F32R)
        part_lo = sb("part_lo", [P, PART_SLOTS, COLS], F32R)
        mid_product = sb("mid_product", [P, COLS])
        middle = sb("middle", [P, COLS], F32R)
        w1_sb = sb("w1_sb", [P, CHUNKS1, P])
        w1c_sb = sb("w1c_sb", [P, P])
        w1c_parts = sb("w1c_parts", [P, P], F32R)
        w2_sb = sb("w2_sb", [P, CHUNKS2, P])
        w2_hi = sb("w2_hi", [P, len(SPLIT2), P], F32R)
        w2_lo = sb("w2_lo", [P, len(SPLIT2), P], F32R)
        b1_sb = sb("b1_sb", [P, 1])
        b2_sb = sb("b2_sb", [P, 1])
        za = sb("za", [P, BATCH])
        zb = sb("zb", [P, BATCH])
        bt1_sb = sb("bt1_sb", [P, TOP1 // P])
        bt2_sb = sb("bt2_sb", [P, TOP2 // P])
        wt3_sb = sb("wt3_sb", [P, TOP2 // P])
        w1b_sb = product[:, PRODUCT_SLOTS - 1, 0:CHUNKS1 * P].rearrange("p (j o) -> p j o", o=P)
        wa_sb = rot[:, 0, 0, 0:TOP1]
        wb_sb = rot[:, 0, 0, TOP1:2 * TOP1]
        wt2_sb = rot[:, 0, 1, :].rearrange("p (u v) -> p u v", v=TOP2)
        top1 = plain1[:, 0:2, :].rearrange("p a c -> p (a c)").rearrange("p (u b) -> p u b", u=TOP1 // P)
        top2 = plain1[:, 2, :].rearrange("p (u b) -> p u b", u=TOP2 // P)

        y_sb = plain1[0:1, 3, 0:BATCH]

        acc1 = ps("acc1", [P, COLS])
        acc2 = ps("acc2", [P, COLS])
        hid = ps("hid", [P, 2, COLS])

        top1_acc = [acc2[:, 0:BANK], acc2[:, BANK:], hid[:, 0, 0:BANK], hid[:, 0, BANK:]]
        top2_acc = [hid[:, 1, 0:BANK], hid[:, 1, BANK:]]

        ids_loaded = sem("ids_loaded")
        rows_ready = sem("rows_ready")
        rows_taken = sem("rows_taken")
        waits_passed = sem("waits_passed")
        fetch_done = [sem(f"fetch_done{i}") for i in range(2)]
        spread_done = [sem(f"spread_done{i}") for i in range(2)]
        unrot_loaded = [sem(f"unrot_loaded{i}") for i in range(2)]
        rot_a_loaded = [[sem(f"rot_a_loaded{i}_{j}") for j in range(CHUNKS1 + 1)] for i in range(2)]
        rot_b_loaded = [sem(f"rot_b_loaded{i}") for i in range(2)]
        w1_loaded = sem("w1_loaded")
        w2_loaded = sem("w2_loaded")
        top_loaded = sem("top_loaded")
        w1_ready = sem("w1_ready")
        w1c_rounded = sem("w1c_rounded")
        w2_rounded = sem("w2_rounded")
        w2_ready = sem("w2_ready")
        plain1_ready = sem("plain1_ready")
        plain1_free = sem("plain1_free")
        plain2_ready = sem("plain2_ready")
        plain2_free = sem("plain2_free")
        mid_product_ready = sem("mid_product_ready")
        mid_hi_ready = sem("mid_hi_ready")
        middle_ready = sem("middle_ready")
        product_ready = sem("product_ready")
        hi_ready = sem("hi_ready")
        lo_by_vector = sem("lo_by_vector")
        lo_by_pool = sem("lo_by_pool")
        parts_free = sem("parts_free")
        acc1_done = sem("acc1_done")
        hid_ready = [sem(f"hid_ready{a}") for a in range(2)]
        sums1_ready = sem("sums1_ready")
        sums2_ready = sem("sums2_ready")
        last_relu_ready = sem("last_relu_ready")
        top1_done = sem("top1_done")
        top1_ready = sem("top1_ready")
        top2_done = sem("top2_done")
        top2_ready = sem("top2_ready")
        top3_done = sem("top3_done")
        y_ready = sem("y_ready")
        y_stored = sem("y_stored")

        N1, N2 = CHUNKS1, CHUNKS2 - len(SPLIT2)
        S2 = len(SPLIT2)

        def layer2_plain_upto(c):
            return sum(x not in SPLIT2 for x in range(c + 1))

        SP2 = len(SPLIT2) - len(VECTOR_LOW_AFTER)

        def vector_low_after(t):
            return LAST_VECTOR_LOW_AFTER if isinstance(t, int) and t == TILES - 1 else VECTOR_LOW_AFTER

        def by_pool(t):
            return [c for c in SPLIT2 if c not in vector_low_after(t)]

        def parts_made(eng, t, k, before=0):
            t, k = (t, k - before) if k >= before else (t - 1, k - before + S2)
            c = SPLIT2[k]
            if c in by_pool(t):
                eng.wait_ge(lo_by_pool, SP2 * t + by_pool(t).index(c) + 1)
            else:
                eng.wait_ge(lo_by_vector, (S2 - SP2) * t + sorted(vector_low_after(t)).index(c) + 1)

        def chunk_made(eng, t, c):
            if c in SPLIT2:
                eng.wait_ge(product_ready, S2 * t + SPLIT2.index(c) + 1)
            else:
                eng.wait_ge(plain2_ready, N2 * t + layer2_plain_upto(c))

        block = ctx.enter_context(nc.Block())

        @block.gpsimd
        def _(pool):
            pool.wait_ge(ids_loaded, 32)
            nc.gpsimd.tensor_tensor(rows_sb[:], ids_sb[:], rows_sb[:], ALU.add).then_inc(rows_ready, 1)
            pool.wait_ge(rows_ready, 1)

            def rows_of(t, par, turn):
                if not (isinstance(turn, int) and turn == 0):
                    pool.wait_ge(spread_done[par], 32 * turn)
                    pool.sem_inc(waits_passed, 1)
                nc.gpsimd.tensor_copy(rows_now[:, par, :], rows_sb[:, bass.ds(t * GATHERS, GATHERS)]).then_inc(rows_taken, 1)
                pool.wait_ge(rows_taken, t + 1)
                pool.sem_inc(waits_passed, 1)

            def fetch(par, g):
                nc.gpsimd.indirect_dma_start(
                    out=fetched[:, par, g * DIM:(g + 1) * DIM], out_offset=None, in_=tables,
                    in_offset=bass.IndirectOffsetOnAxis(ap=rows_now[:, par, g:g + 1], axis=0),
                ).then_inc(fetch_done[par], 16)

            def step(t, par, turn, fetching=True):
                if fetching:
                    rows_of(t + 3, 1 - par, turn)
                for n, c in enumerate(by_pool(t)):
                    k = SPLIT2.index(c)
                    pool.wait_ge(hi_ready, S2 * t + k + 1)
                    nc.gpsimd.tensor_tensor(part_lo[:, (S2 * par + k) % PART_SLOTS, :],
                                            product[:, (S2 * par + k) % PRODUCT_SLOTS, :],
                                            part_hi[:, (S2 * par + k) % PART_SLOTS, :].bitcast(F32),
                                            ALU.subtract).then_inc(lo_by_pool, 1)
                    if fetching and n in FETCH_AFTER:
                        fetch(1 - par, FETCH_AFTER.index(n))

            for t in range(3):
                rows_of(t, t % 2, t // 2)
                for g in range(GATHERS):
                    fetch(t % 2, g)
            step(0, 0, 1)
            with pool.Fori(0, (TILES - 4) // 2) as i:
                step(2 * i + 1, 1, i + 2)
                step(2 * i + 2, 0, i + 2)
            for t in range(TILES - 3, TILES):
                step(t, t % 2, None, fetching=False)

        @block.sync
        def _(sp):
            sp.dma_start(ids_sb[:], ids).then_inc(ids_loaded, 16)

            def spread(t, par, turn):
                sp.wait_ge(fetch_done[par], 16 * GATHERS * (turn + 1))
                for half in range(2):
                    dst = scratch[bass.ds(t, 1), half * FIELDS:(half + 1) * FIELDS, :]
                    sp.dma_start(dst.rearrange("o m (s c) -> (o m) s c", s=PER_GATHER),
                                 fetched[:, par, :]).then_inc(spread_done[par], 16)

            def rotated(t, first_row, quad_step):
                rows = scratch[bass.ds(t, 1), first_row:first_row + FIELDS, :].rearrange("o m c -> (o m) c")
                return bass.AP(tensor=rows.tensor, offset=rows.offset,
                               ap=[[quad_step * COLS, P // QUAD], [COLS, QUAD], [1, COLS]])

            def load1(t, par, turn):
                sp.wait_ge(spread_done[par], 32 * (turn + 1))
                sp.sem_inc(waits_passed, 1)
                if not (isinstance(t, int) and t == 0):
                    sp.wait_ge(plain1_ready, N1 * t)
                    sp.sem_inc(waits_passed, 1)
                    sp.wait_ge(mid_product_ready, t)
                sp.dma_start(unrot[:], rotated(t, 0, 0)).then_inc(unrot_loaded[par], 16)
                mid_last = isinstance(t, int) and t == 0
                if not mid_last:
                    sp.dma_start(rot16[:], rotated(t, 16, 0)).then_inc(rot_a_loaded[par][CHUNKS1], 16)
                for j in range(CHUNKS1):
                    if not (isinstance(t, int) and t < 2):
                        chunk_made(sp, t - 2, ROTS + j)
                    sp.dma_start(rot[:, par, j, :], rotated(t, 4 * j, 1)).then_inc(rot_a_loaded[par][j], 16)
                if mid_last:
                    sp.dma_start(rot16[:], rotated(t, 16, 0)).then_inc(rot_a_loaded[par][CHUNKS1], 16)

            def load2(t, par):
                for j in range(CHUNKS1, ROTS):
                    if not (isinstance(t, int) and t < 2):
                        chunk_made(sp, t - 2, ROTS + j)
                    sp.dma_start(rot[:, par, j, :], rotated(t, 4 * j, 1)).then_inc(rot_b_loaded[par], 16)

            def load(t, par, turn):
                spread(t, par, turn)
                load1(t, par, turn)
                load2(t, par)

            spread(0, 0, 0)
            load1(0, 0, 0)
            spread(1, 1, 0)
            load2(0, 0)
            load1(1, 1, 0)
            load2(1, 1)
            load(2, 0, 1)
            with sp.Fori(1, TILES // 2 - 1) as i:
                load(2 * i + 1, 1, i)
                load(2 * i + 2, 0, i + 1)
            load(TILES - 1, 1, TILES // 2 - 1)
            sp.wait_ge(y_ready, 1)
            sp.dma_start(y, y_sb).then_inc(y_stored, 16)
            sp.wait_ge(y_stored, 16)

        @block.vector
        def _(dve):
            dve.wait_ge(w1_loaded, 64)
            nc.vector.tensor_tensor(w1_sb[:], w1_sb[:], w1b_sb, ALU.add).then_inc(w1_ready, 1)
            dve.wait_ge(w1c_rounded, 1)
            for q in (1, 3):
                at = slice(q * QUAD, (q + 1) * QUAD)
                nc.vector.tensor_tensor(w1c_parts[at, :], w1c_sb[at, :], w1c_parts[at, :].bitcast(F32),
                                        ALU.subtract).then_inc(w1_ready, 1)

            def split_weights():
                for k, c in enumerate(SPLIT2):
                    dve.wait_ge(w2_rounded, k + 1)
                    nc.vector.tensor_tensor(w2_lo[:, k, :], w2_sb[:, c, :], w2_hi[:, k, :].bitcast(F32),
                                            ALU.subtract).then_inc(w2_ready, 1)

            def layer1(t, par, turn, j, first=False):
                if j in (0, CHUNKS1):
                    dve.wait_ge(unrot_loaded[par], 16 * (turn + 1))
                if j == CHUNKS1:
                    dve.wait_ge(rot_a_loaded[par][j], 16 * (turn + 1))
                    if not first:
                        dve.wait_ge(middle_ready, t)
                    nc.vector.tensor_tensor(mid_product[:], unrot[:], rot16[:],
                                            ALU.mult).then_inc(mid_product_ready, 1)
                else:
                    dve.wait_ge(rot_a_loaded[par][j], 16 * (turn + 1))
                    if not first:
                        dve.wait_ge(plain1_free, N1 * (t - 1) + j + 1)
                    nc.vector.tensor_tensor(plain1[:, j, :], unrot[:], rot[:, par, j, :],
                                            ALU.mult).then_inc(plain1_ready, 1)

            def middle_low(t):
                dve.wait_ge(mid_hi_ready, t + 1)
                at = slice(P // 2, P)
                nc.vector.tensor_tensor(middle[at, :], mid_product[at, :], middle[at, :].bitcast(F32),
                                        ALU.subtract).then_inc(middle_ready, 1)

            def step(t, par, turn, first=False, layer1_too=True):
                s, s_at, n_at = S2 * t, S2 * par, N2 * par
                np_ = 0
                for c in range(CHUNKS2):
                    arr, j = c // ROTS, c % ROTS
                    if j == 0:
                        dve.wait_ge(hid_ready[arr], t + 1)
                    if c == CHUNKS1:
                        dve.wait_ge(rot_b_loaded[par], 16 * (ROTS - CHUNKS1) * (turn + 1))
                    if c in SPLIT2:
                        k = SPLIT2.index(c)
                        if not (isinstance(t, int) and S2 * t + k < PRODUCT_SLOTS):
                            parts_made(dve, t, k, before=PRODUCT_SLOTS)
                        out, ready = product[:, (s_at + k) % PRODUCT_SLOTS, :], product_ready
                    else:
                        dve.wait_ge(plain2_free, N2 * t + np_ + 1)
                        out, ready = plain2[:, (n_at + np_) % PLAIN2_SLOTS, :], plain2_ready
                        np_ += 1
                    nc.vector.tensor_tensor(out, hid[:, arr, :], rot[:, par, j, :],
                                            ALU.mult).then_inc(ready, 1)
                    if first and c in START_LAYER1_AFTER:
                        layer1(1, 1, 0, START_LAYER1_AFTER[c])
                    if first and c == START_MIDDLE_LOW_AFTER:
                        middle_low(1)
                    if c in LAYER1_AFTER and layer1_too:
                        layer1(t + 2, par, turn + 1, LAYER1_AFTER[c])
                    if c == MIDDLE_LOW_AFTER and layer1_too:
                        middle_low(t + 2)
                    for k in (SPLIT2.index(x) for x, after in vector_low_after(t).items() if after == c):
                        dve.wait_ge(hi_ready, s + k + 1)
                        nc.vector.tensor_tensor(part_lo[:, (s_at + k) % PART_SLOTS, :],
                                                product[:, (s_at + k) % PRODUCT_SLOTS, :],
                                                part_hi[:, (s_at + k) % PART_SLOTS, :].bitcast(F32),
                                                ALU.subtract).then_inc(lo_by_vector, 1)

            split_weights()
            for j in (*range(CHUNKS1), CHUNKS1):
                layer1(0, 0, 0, j, first=True)
            middle_low(0)
            step(0, 0, 0, first=True)
            with dve.Fori(0, (TILES - 4) // 2) as i:
                step(2 * i + 1, 1, i)
                step(2 * i + 2, 0, i + 1)
            for t in range(TILES - 3, TILES):
                step(t, t % 2, t // 2, layer1_too=(t + 2 < TILES))
            for b in range(COLS // BANK):
                dve.wait_ge(last_relu_ready, b + 1)
                first_col = (TILES - 1) * SAMPLES + b * BANK // DIM
                done = nc.vector.tensor_reduce(zb[:, first_col:first_col + BANK // DIM],
                                               acc1[:, b * BANK:(b + 1) * BANK].rearrange("p (s d) -> p s d", d=DIM),
                                               AX.X, ALU.add)
            done.then_inc(sums2_ready, 1)

        @block.scalar
        def _(act):
            act.dma_start(rows_sb[:], bases).then_inc(ids_loaded, 16)
            act.dma_start(w1_sb[:], w1a).then_inc(w1_loaded, 16)
            act.dma_start(w1b_sb, w1b).then_inc(w1_loaded, 16)
            act.dma_start(w1c_sb[:], w1c).then_inc(w1_loaded, 16)
            act.dma_start(b1_sb[:], b1).then_inc(w1_loaded, 16)
            act.dma_start(w2_sb[:], w2).then_inc(w2_loaded, 16)
            act.dma_start(b2_sb[:], b2).then_inc(w2_loaded, 16)
            act.wait_ge(w1_loaded, 64)
            nc.scalar.activation(w1c_parts[:], w1c_sb[:], ACT.Copy).then_inc(w1c_rounded, 1)

            def round1(t, first=False):
                act.wait_ge(mid_product_ready, t + 1)
                if not first:
                    act.wait_ge(acc1_done, t)
                nc.scalar.activation(middle[:], mid_product[:], ACT.Copy).then_inc(mid_hi_ready, 1)

            def hidden_rows(t, part, fresh=False):
                if part == 0:
                    act.wait_ge(acc1_done, t + 1)
                if part < 2 and not fresh:
                    chunk_made(act, t - 1, (ROTS - 1, CHUNKS2 - 1)[part])
                if part == 0:
                    moves = ((0, 0, 64, 0), (0, 64, 64, 0))
                elif part == 1:
                    moves = ((32, 0, 32, 1), (0, 32, 32, 1))
                else:
                    moves = ((32, 64, 32, 1), (0, 96, 32, 1))
                for src, dst, rows, arr in moves:
                    done = nc.scalar.activation(hid[dst:dst + rows, arr, :], acc1[src:src + rows, :],
                                                ACT.Relu, bias=b1_sb[src:src + rows, :])
                if part != 1:
                    done.then_inc(hid_ready[part // 2], 1)

            def summed_rows(t, acc, rows, bias, sums, piece):
                for n in range(piece * SAMPLES // 4, (piece + 1) * SAMPLES // 4):
                    at = slice(n * DIM, (n + 1) * DIM)
                    done = nc.scalar.activation(acc[rows, at], acc[rows, at], ACT.Relu, bias=bias[rows, :],
                                                accum_out=sums[rows, bass.ds(t * SAMPLES + n, 1)])
                return done

            def sums1(t, piece):
                done = summed_rows(t, acc1[:], slice(P // 2, P), b1_sb, za, piece)
                if piece == 3:
                    done.then_inc(sums1_ready, 1)

            def sums2(t, piece):
                if piece == 0:
                    act.wait_ge(plain2_free, PLAIN2_SLOTS + N2 * (t + 1))
                done = summed_rows(t, acc2[:], slice(0, P), b2_sb, zb, piece)
                if piece == 3:
                    done.then_inc(sums2_ready, 1)

            def round2(t, par, k):
                n = S2 * t + k
                act.wait_ge(product_ready, n + 1)
                act.wait_ge(parts_free, n + 1)
                nc.scalar.activation(part_hi[:, (S2 * par + k) % PART_SLOTS, :],
                                     product[:, (S2 * par + k) % PRODUCT_SLOTS, :], ACT.Copy).then_inc(hi_ready, 1)

            def step(t, par, first=False, ahead=2):
                if not first:
                    hidden_rows(t, 1)
                    hidden_rows(t, 2)
                if ahead == 0:
                    chunk_made(act, t - 1, CHUNKS2 - 1)
                    act.dma_start(wa_sb, wa).then_inc(top_loaded, 16)
                    act.dma_start(wb_sb, wb).then_inc(top_loaded, 16)
                    act.dma_start(wt2_sb, wt2).then_inc(top_loaded, 16)
                for k, c in enumerate(SPLIT2):
                    round2(t, par, k)
                    for part in (1, 2):
                        if first and c == START_SWAPPED_AFTER[part - 1]:
                            hidden_rows(0, part, fresh=True)
                    if first and c == START_ROUND1_AFTER:
                        round1(1)
                    for piece in range(4):
                        if first and c == START_SUMS1_AFTER[piece]:
                            sums1(0, piece)
                    for piece in range(4):
                        if not first and c == SUMS2_AFTER[piece]:
                            sums2(t - 1, piece)
                        if ahead > 0 and c == SUMS1_AFTER[piece]:
                            sums1(t + 1, piece)
                    if ahead > 0 and c == HIDDEN_AFTER:
                        hidden_rows(t + 1, 0)
                    if ahead > 1 and c == ROUND1_AFTER:
                        round1(t + 2)

            act.wait_ge(w2_loaded, 32)
            for k, c in enumerate(SPLIT2):
                nc.scalar.activation(w2_hi[:, k, :], w2_sb[:, c, :], ACT.Copy).then_inc(w2_rounded, 1)
            round1(0, first=True)
            hidden_rows(0, 0, fresh=True)
            step(0, 0, first=True)
            act.dma_start(za[0:P // 2, :], dense_t).then_inc(top_loaded, 16)
            act.dma_start(bt1_sb[:], bt1).then_inc(top_loaded, 16)
            act.dma_start(bt2_sb[:], bt2).then_inc(top_loaded, 16)
            act.dma_start(wt3_sb[:], wt3).then_inc(top_loaded, 16)
            with act.Fori(0, (TILES - 4) // 2) as i:
                step(2 * i + 1, 1)
                step(2 * i + 2, 0)
            for t in range(TILES - 3, TILES):
                step(t, t % 2, ahead=TILES - 1 - t)
            act.wait_ge(plain2_free, PLAIN2_SLOTS + N2 * TILES)
            for b in range(COLS // BANK):
                at = slice(b * BANK, (b + 1) * BANK)
                nc.scalar.activation(acc1[:, at], acc1[:, at], ACT.Relu, bias=b2_sb[:]).then_inc(last_relu_ready, 1)

            for u in range(TOP1 // P):
                act.wait_ge(top1_done, u + 1)
                if u == 0:
                    act.wait_ge(top_loaded, 112)
                nc.scalar.activation(top1[:, u, :], top1_acc[u], ACT.Relu,
                                     bias=bt1_sb[:, u:u + 1]).then_inc(top1_ready, 1)
            for u in range(TOP2 // P):
                act.wait_ge(top2_done, u + 1)
                nc.scalar.activation(top2[:, u, :], top2_acc[u], ACT.Relu,
                                     bias=bt2_sb[:, u:u + 1]).then_inc(top2_ready, 1)
            act.wait_ge(top3_done, 1)
            nc.scalar.activation(y_sb, acc1[0:1, 0:BANK], ACT.Copy).then_inc(y_ready, 1)

        @block.tensor
        def _(pe):
            pe.sem_inc(plain2_free, PLAIN2_SLOTS)
            pe.sem_inc(parts_free, PART_SLOTS)
            banks = [slice(b * BANK, (b + 1) * BANK) for b in range(COLS // BANK)]

            def layer1(t, first=False):
                if not first:
                    pe.wait_ge(hid_ready[1], t)
                    pe.wait_ge(sums1_ready, t)
                for j in range(CHUNKS1):
                    pe.wait_ge(plain1_ready, N1 * t + j + 1)
                    for at in banks:
                        done = nc.tensor.matmul(acc1[:, at], w1_sb[:, j, :], plain1[:, j, at],
                                                start=(j == 0), stop=False)
                    done.then_inc(plain1_free, 1)
                pe.wait_ge(middle_ready, t + 1)
                for at in banks:
                    done = nc.tensor.matmul(acc1[:, at], w1c_parts[:], middle[:, at], start=False, stop=True)
                done.then_inc(acc1_done, 1)

            def layer2(t, par, acc=acc2, chunks=range(CHUNKS2)):
                n, n_at, s_at = N2 * t, N2 * par, S2 * par
                np_ = sum(c not in SPLIT2 for c in range(chunks[0]))
                if acc is acc1:
                    pe.wait_ge(hid_ready[1], t + 1)
                    pe.wait_ge(sums1_ready, t + 1)
                elif not (isinstance(t, int) and t == 0):
                    pe.wait_ge(sums2_ready, t)
                for c in chunks:
                    if c in SPLIT2:
                        k = SPLIT2.index(c)
                        slot = (s_at + k) % PART_SLOTS
                        parts_made(pe, t, k)
                        for w, parts in ((w2_hi, part_hi), (w2_hi, part_lo), (w2_lo, part_hi)):
                            for at in banks:
                                done = nc.tensor.matmul(acc[:, at], w[:, k, :], parts[:, slot, at],
                                                        start=False, stop=False)
                        done.then_inc(parts_free, 1)
                    else:
                        pe.wait_ge(plain2_ready, n + np_ + 1)
                        for at in banks:
                            done = nc.tensor.matmul(acc[:, at], w2_sb[:, c, :],
                                                    plain2[:, (n_at + np_) % PLAIN2_SLOTS, at],
                                                    start=(c == 0), stop=(c == CHUNKS2 - 1))
                        np_ += 1
                        done.then_inc(plain2_free, 1)

            pe.wait_ge(w1_ready, 3)
            layer1(0, first=True)
            pe.wait_ge(w2_ready, S2)
            layer2(0, 0, chunks=range(START_CHUNKS))
            layer1(1)
            layer2(0, 0, chunks=range(START_CHUNKS, CHUNKS2))
            with pe.Fori(0, TILES // 2 - 1) as i:
                layer1(2 * i + 2)
                layer2(2 * i + 1, 1)
                layer1(2 * i + 3)
                layer2(2 * i + 2, 0)
            layer2(TILES - 1, 1, acc=acc1, chunks=range(TOP_AFTER_CHUNKS))

            def top1_first(u):
                nc.tensor.matmul(top1_acc[u], wa_sb[:, u * P:(u + 1) * P], za[:], start=True, stop=False)

            pe.wait_ge(top_loaded, 112)
            pe.wait_ge(sums2_ready, TILES - 1)
            top1_first(0)
            top1_first(1)
            layer2(TILES - 1, 1, acc=acc1, chunks=range(TOP_AFTER_CHUNKS, CHUNKS2))
            chunk_made(pe, TILES - 1, CHUNKS2 - 1)
            top1_first(2)
            top1_first(3)
            pe.wait_ge(sums2_ready, TILES)
            for u in range(TOP1 // P):
                nc.tensor.matmul(top1_acc[u], wb_sb[:, u * P:(u + 1) * P], zb[:], start=False,
                                 stop=True).then_inc(top1_done, 1)
            for u in range(TOP1 // P):
                pe.wait_ge(top1_ready, u + 1)
                for v in range(TOP2 // P):
                    done = nc.tensor.matmul(top2_acc[v], wt2_sb[:, u, v * P:(v + 1) * P],
                                            top1[:, u, :], start=(u == 0), stop=(u == TOP1 // P - 1))
                    if u == TOP1 // P - 1:
                        done.then_inc(top2_done, 1)
            for u in range(TOP2 // P):
                pe.wait_ge(top2_ready, u + 1)
                done = nc.tensor.matmul(acc1[0:1, 0:BANK], wt3_sb[:, u:u + 1], top2[:, u, :],
                                        start=(u == 0), stop=(u == TOP2 // P - 1))
            done.then_inc(top3_done, 1)


def kernel(**inputs):
    import numpy as np
    import concourse.bacc as bacc
    from concourse import mybir as mb
    from concourse.bass_utils import run_bass_kernel_spmd as run

    x = {name: np.asarray(a) for name, a in inputs.items()}
    tables = [x[f"tbl_{f}"] for f in range(FIELDS)]
    starts = np.concatenate([[0], np.cumsum([t.shape[0] for t in tables])[:-1]]).astype(np.int32)
    ids = x["ids"].reshape(TILES, PER_GATHER, GATHERS, FIELDS).transpose(3, 1, 0, 2).reshape(P, -1)
    bases = np.broadcast_to(starts[:, None, None], (FIELDS, PER_GATHER, TILES * GATHERS)).reshape(P, -1)

    q, p = np.repeat(np.arange(4), QUAD), np.tile(np.arange(QUAD), 4)
    other = (p[:, None] + 4 * np.arange(ROTS)[None, :] + q[:, None]) % FIELDS
    w1 = x["L0_rec_W1"].reshape(P, FIELDS, FIELDS)
    w1a = w1[:, p[:, None], other[:, :CHUNKS1]].transpose(1, 2, 0)
    w1b = w1[:, other[:, :CHUNKS1], p[:, None]].transpose(1, 2, 0).copy()
    w1b[0:QUAD, 0, :] = 0
    w1c = w1[:, p, (p + 16) % FIELDS].T
    w2 = x["L0_rec_W2"].reshape(P, HIDDEN, FIELDS)
    arr = np.arange(2)[None, :, None]
    hidden = p[:, None, None] + QUAD * ((q[:, None, None] + arr) % 2) + 0 * other[:, None, :]
    w2 = w2[:, hidden, other[:, None, :] + 0 * arr].reshape(P, P, CHUNKS2).transpose(1, 2, 0)

    top = x["W_top1"]
    cin = DIRECT1 + OUT2
    gap = np.zeros((P // 2 - DENSE, TOP1), np.float32)
    dense_t = np.concatenate([x["dense_ctx"].T, np.zeros((P // 2 - DENSE, BATCH), np.float32)])
    laid = {
        "tables": np.concatenate(tables),
        "ids": ids,
        "bases": bases,
        "w1a": w1a,
        "w1b": w1b,
        "w1c": w1c,
        "b1": x["L0_rec_b1"].reshape(P, 1),
        "w2": w2,
        "b2": x["L0_rec_b2"].reshape(P, 1),
        "dense_t": dense_t,
        "wa": np.concatenate([top[cin:], gap, top[:DIRECT1]]),
        "wb": top[DIRECT1:cin],
        "bt1": x["b_top1"].reshape(-1, P).T,
        "wt2": x["W_top2"].reshape(-1, P, TOP2).transpose(1, 0, 2),
        "bt2": x["b_top2"].reshape(-1, P).T,
        "wt3": x["W_top3"].reshape(-1, P).T,
    }
    nc = bacc.Bacc("TRN2", target_bir_lowering=False, num_devices=1)
    arrays, args = {}, []
    for name, a in laid.items():
        a = np.ascontiguousarray(a)
        arrays[f"in_{name}"] = a
        args.append(nc.dram_tensor(f"in_{name}", a.shape, mb.dt.from_np(a.dtype), kind="ExternalInput").ap())
    out = nc.dram_tensor("out_y", (1, BATCH), mb.dt.float32, kind="ExternalOutput").ap()
    cin_tower(nc, *args, out)
    r = run(nc, [arrays], core_ids=[0])
    return r.results[0]["out_y"].reshape(BATCH, 1)
```
